# Optimizing a Trainium2 kernel written in Bass

```python
import numpy as np
import jax
import jax.numpy as jnp

def _softmax(x, axis=-1):
    return jax.nn.softmax(x, axis=axis)

def _gelu(x):
    return jax.nn.gelu(x, approximate=True)

def _silu(x):
    return jax.nn.silu(x)

def _sigmoid(x):
    return jax.nn.sigmoid(x)

def _layernorm(x, axis=-1, eps=1e-05):
    m = jnp.mean(x, axis=axis, keepdims=True)
    v = jnp.var(x, axis=axis, keepdims=True)
    return (x - m) / jnp.sqrt(v + eps)

def _scatter_add(tgt, idx, src, axis=0):
    return tgt.at[idx].add(src)

def _segment_sum(src, seg, n):
    return jax.ops.segment_sum(src, seg, n)
kernel_name = 'mk_prb_d1_jaxref_r8_89fa24'

def setup_inputs(seed: int=0):
    np.random.seed(seed)
    _w = jnp.asarray

    def _L0_attn_setup():
        import jax, jax.numpy as jnp
        import numpy as np
        H = 32
        G = 8
        D = 128
        HID = 512
        THETA = 10000.0

        def _rope(x, pos):
            half = D // 2
            inv_freq = 1.0 / THETA ** (jnp.arange(0, half, dtype=jnp.float32) / half)
            ang = pos[:, None].astype(jnp.float32) * inv_freq[None, :]
            cos = jnp.cos(ang)[None, None]
            sin = jnp.sin(ang)[None, None]
            x1, x2 = (x[..., :half], x[..., half:])
            return jnp.concatenate([x1 * cos - x2 * sin, x1 * sin + x2 * cos], axis=-1)
        key = jax.random.key(seed)
        ks = jax.random.split(key, 9)
        s = 0.02
        return {'hidden_states': jax.random.normal(ks[0], (1, 256, HID), jnp.float32), 'Wq': jax.random.normal(ks[1], (HID, H * D), jnp.float32) * s, 'bq': jnp.zeros((H * D,), jnp.float32), 'Wk': jax.random.normal(ks[2], (HID, G * D), jnp.float32) * s, 'bk': jnp.zeros((G * D,), jnp.float32), 'Wv': jax.random.normal(ks[3], (HID, G * D), jnp.float32) * s, 'bv': jnp.zeros((G * D,), jnp.float32), 'Wo': jax.random.normal(ks[4], (H * D, HID), jnp.float32) * s, 'bo': jnp.zeros((HID,), jnp.float32)}
    _L0_attn_in = _L0_attn_setup()

    def _L0_ffn_setup():
        import jax, jax.numpy as jnp
        import numpy as np
        MAX_THRESHOLD = 1.0 / 8.0
        SCALING = 32.0 / 16.0
        key = jax.random.key(seed)
        ks = jax.random.split(key, 8)
        B_, S, D, O, E, R = (4, 256, 512, 512, 8, 16)
        sd = 1.0 / np.sqrt(D)
        return {'x': jax.random.normal(ks[0], (B_, S, D), jnp.float32), 'W_base': jax.random.normal(ks[1], (O, D), jnp.float32) * sd, 'b_base': jax.random.normal(ks[2], (O,), jnp.float32) * 0.01, 'W_gate': jax.random.normal(ks[3], (E, D), jnp.float32) * sd, 'W_thr': jax.random.normal(ks[4], (1, D), jnp.float32) * sd, 'b_thr': jax.random.normal(ks[5], (1,), jnp.float32) * 0.01, 'A': jax.random.normal(ks[6], (E, R, D), jnp.float32) * sd, 'B': jax.random.normal(ks[7], (O,), jnp.float32)[None, :, None] * jnp.zeros((E, O, R), jnp.float32) + jax.random.normal(jax.random.fold_in(key, 7), (E, O, R), jnp.float32) * (1.0 / np.sqrt(R))}
    _L0_ffn_in = _L0_ffn_setup()
    _d = {'L0_attn_hidden_states': _L0_attn_in['hidden_states'], 'L0_attn_Wq': _L0_attn_in['Wq'], 'L0_attn_bq': _L0_attn_in['bq'], 'L0_attn_Wk': _L0_attn_in['Wk'], 'L0_attn_bk': _L0_attn_in['bk'], 'L0_attn_Wv': _L0_attn_in['Wv'], 'L0_attn_bv': _L0_attn_in['bv'], 'L0_attn_Wo': _L0_attn_in['Wo'], 'L0_attn_bo': _L0_attn_in['bo'], 'L0_ffn_W_base': _L0_ffn_in['W_base'], 'L0_ffn_b_base': _L0_ffn_in['b_base'], 'L0_ffn_W_gate': _L0_ffn_in['W_gate'], 'L0_ffn_W_thr': _L0_ffn_in['W_thr'], 'L0_ffn_b_thr': _L0_ffn_in['b_thr'], 'L0_ffn_A': _L0_ffn_in['A'], 'L0_ffn_B': _L0_ffn_in['B']}
    _x0 = _d['L0_attn_hidden_states']
    _d['L0_attn_hidden_states'] = jax.random.normal(jax.random.fold_in(jax.random.key(seed), 1), (2, 1024, 512), dtype=_x0.dtype)
    del _x0
    return _d

def reference(L0_attn_hidden_states, L0_attn_Wq, L0_attn_bq, L0_attn_Wk, L0_attn_bk, L0_attn_Wv, L0_attn_bv, L0_attn_Wo, L0_attn_bo, L0_ffn_W_base, L0_ffn_b_base, L0_ffn_W_gate, L0_ffn_W_thr, L0_ffn_b_thr, L0_ffn_A, L0_ffn_B):

    def _L0_attn_ref(hidden_states, Wq, bq, Wk, bk, Wv, bv, Wo, bo):
        import jax, jax.numpy as jnp
        import numpy as np
        H = 32
        G = 8
        D = 128
        HID = 512
        THETA = 10000.0

        def _rope(x, pos):
            half = D // 2
            inv_freq = 1.0 / THETA ** (jnp.arange(0, half, dtype=jnp.float32) / half)
            ang = pos[:, None].astype(jnp.float32) * inv_freq[None, :]
            cos = jnp.cos(ang)[None, None]
            sin = jnp.sin(ang)[None, None]
            x1, x2 = (x[..., :half], x[..., half:])
            return jnp.concatenate([x1 * cos - x2 * sin, x1 * sin + x2 * cos], axis=-1)
        B, S, _ = hidden_states.shape
        R = H // G
        q = hidden_states @ Wq + bq
        k = hidden_states @ Wk + bk
        v = hidden_states @ Wv + bv
        q = q.reshape(B, S, H, D).transpose(0, 2, 1, 3)
        k = k.reshape(B, S, G, D).transpose(0, 2, 1, 3)
        v = v.reshape(B, S, G, D).transpose(0, 2, 1, 3)
        pos = jnp.arange(S)
        q = _rope(q, pos)
        k = _rope(k, pos)
        qg = q.reshape(B, G, R, S, D)
        scores = jnp.einsum('bgrsd,bgtd->bgrst', qg, k) / jnp.sqrt(jnp.float32(D))
        causal = jnp.tril(jnp.ones((S, S), dtype=bool))
        scores = jnp.where(causal[None, None, None], scores, jnp.finfo(scores.dtype).min)
        probs = jax.nn.softmax(scores, axis=-1)
        ctx = jnp.einsum('bgrst,bgtd->bgrsd', probs, v)
        ctx = ctx.reshape(B, H, S, D).transpose(0, 2, 1, 3).reshape(B, S, H * D)
        return ctx @ Wo + bo

    def _L0_ffn_ref(x, W_base, b_base, W_gate, W_thr, b_thr, A, B):
        import jax, jax.numpy as jnp
        import numpy as np
        MAX_THRESHOLD = 1.0 / 8.0
        SCALING = 32.0 / 16.0
        base = jnp.einsum('bsd,od->bso', x, W_base) + b_base
        D = x.shape[-1]
        xf = x.reshape(-1, D)
        gate_logits = jax.nn.softmax(xf @ W_gate.T, axis=-1)
        thresholds = jax.nn.sigmoid(xf @ W_thr.T + b_thr) * MAX_THRESHOLD
        adapted = gate_logits - thresholds
        selected = (adapted >= 0).astype(x.dtype)
        weights = adapted * selected
        wsum = jnp.sum(weights, axis=-1, keepdims=True)
        wsum = jnp.where(wsum == 0, jnp.ones_like(wsum), wsum)
        weights = weights / wsum
        h = jnp.einsum('nd,erd->ner', xf, A)
        moe = jnp.einsum('ner,ne,eor->no', h, weights, B) * SCALING
        out = base + moe.reshape(base.shape)
        return out
    x = L0_attn_hidden_states
    xn = _layernorm(x, axis=-1)
    x = x + _L0_attn_ref(xn, L0_attn_Wq, L0_attn_bq, L0_attn_Wk, L0_attn_bk, L0_attn_Wv, L0_attn_bv, L0_attn_Wo, L0_attn_bo) + _L0_ffn_ref(xn, L0_ffn_W_base, L0_ffn_b_base, L0_ffn_W_gate, L0_ffn_W_thr, L0_ffn_b_thr, L0_ffn_A, L0_ffn_B)
    return x

_drawn_inputs = setup_inputs


def setup_inputs(seed=0):
    import zlib

    import numpy as np

    out = dict(_drawn_inputs(seed))
    spreads = {'L0_attn_bq': (0.0, 0.8),
     'L0_attn_bk': (0.0, 0.8),
     'L0_attn_bv': (0.0, 0.1),
     'L0_attn_bo': (0.0, 0.1)}
    factors = {'L0_attn_Wq': 8.0, 'L0_attn_Wk': 8.0, 'L0_ffn_b_base': 8.0}
    for name, (base, spread) in spreads.items():
        noise = np.random.default_rng([zlib.crc32(name.encode()), seed]).standard_normal(out[name].shape)
        drawn = base * np.exp(spread * noise) if base else spread * noise
        out[name] = jnp.asarray(drawn.astype(out[name].dtype))
    for name, factor in factors.items():
        out[name] = (out[name] * factor).astype(out[name].dtype)
    return out
```

```python
import concourse.bass as bass
from concourse import mybir
from contextlib import ExitStack

B, S, HID = 2, 1024, 512
H, GROUPS, D = 32, 8, 128
RH = H // GROUPS
E, R = 8, 16
P = 128
KT = HID // P
ST = S // P
CH = 512
TC = CH // P
SLOTS = TC + ST
LAG = 2
PART_LAG = 2
OUT_SLOTS = ((0, 2, 7, 8, 9, 10), (8, 9))
NGATE = E * R + E + 2
NB = RH + 2
EPS = 1e-5
MAX_THR = 1.0 / 8.0
SCALING = 2.0
UNITS = 2 * RH + 2
PRE_UNITS = 4


def chunk_block(s):
    return (0, s) if s < TC else (1, s - TC)


def block_start(s):
    c, j = chunk_block(s)
    return max(j - TC * c, 0) * P


def score_tile(s):
    if s < 3:
        return False, TC + 1 + s
    if 7 <= s < 11:
        return True, s - 7
    if s == 11:
        return True, TC
    return None


def units_of(r, s, has_prev, has_next):
    found = []
    if s in (1, 11):
        found.append(("rinv", r, s // 11))
    if r == 0 and s == 6:
        found.append(("vturn", 1))
    if r < RH - 1:
        if s in (3, 5):
            found.append(("proj", PRE_UNITS + 2 * r + (s == 5)))
    elif has_next and s in (2, 3, 5, 7):
        found.append(("proj", PRE_UNITS + 2 * r + s // 2 - (s == 2)))
    if r == 1 and has_next and s in (6, 7):
        found.append(("vproj", s - 4))
    if r == RH - 1 and has_next and s == 10:
        found.append(("vturn", 2))
    if r >= 2 or has_prev:
        slots = OUT_SLOTS[r % 2]
        if s in slots:
            found.append(("out", 0 if r >= 2 else -1,
                          (len(OUT_SLOTS[0]) if r % 2 else 0) + slots.index(s)))
    return found


def proj_target(j):
    ahead, j = divmod(j, UNITS)
    if j < PRE_UNITS:
        return ("k", "q")[j % 2], j // 2, ahead * RH
    return "q", j % 2, (j - PRE_UNITS) // 2 + 1 + ahead * RH


def build(nc, x, wq, wk, wv, wo, bqkv, bo, wbase, bbase, wgate, bthr, badapt, tables, out):
    f32, f32r, bf16 = mybir.dt.float32, mybir.dt.float32r, mybir.dt.bfloat16
    ALU = mybir.AluOpType
    ACT = mybir.ActivationFunctionType
    AX = mybir.AxisListType
    ctx = ExitStack()
    with ctx:
        def sb(name, shape, dt=f32):
            return ctx.enter_context(nc.sbuf_tensor(name, shape, dt))

        def sem(name):
            return ctx.enter_context(nc.semaphore(name))

        HI, LO = 0, 1
        xnT = sb("xnT", [P, 2, KT, S], f32r)
        kT = sb("kT", [P, 2, S], f32r)
        qT = sb("qT", [P, 2, S], f32r)
        v = sb("v", [P, 2, ST, D], f32r)
        ctxT = sb("ctxT", [P, 2, RH, S], f32r)
        acc = sb("acc", [P, ST, HID])
        prob = sb("prob", [P, TC * CH + TC * S])
        probT = sb("probT", [P, LAG, 2, CH], f32r)
        wo_parts = sb("wo_parts", [P, 2, 2, 2, HID], f32r)
        wq_parts = sb("wq_parts", [P, 2, KT, D], f32r)
        wk_parts = sb("wk_parts", [P, 2, KT, D], f32r)
        wv_parts = sb("wv_parts", [P, 2, KT, D], f32r)
        wq_raw = sb("wq_raw", [P, KT, D])
        wk_raw = sb("wk_raw", [P, KT, D])
        wv_raw = sb("wv_raw", [P, KT, D])
        wo_raw = sb("wo_raw", [P, 2, HID])
        biased = sb("biased", [P, 2, CH])
        rotated = sb("rotated", [P, 2, CH])
        crossed = sb("crossed", [P, 2, CH])
        vT = sb("vT", [P, S])
        rinv_wide = sb("rinv_wide", [P, 2, CH])
        normed = sb("normed", [P, CH])
        cos_sin = sb("cos_sin", [P, 2, S])
        ident = sb("ident", [P, P])
        ident_b = sb("ident_b", [P, P], bf16)
        mask = sb("mask", [P, P])
        mask_b = sb("mask_b", [P, P], bf16)
        bias = sb("bias", [P, GROUPS * NB + 3])
        bias_now = sb("bias_now", [P, NB])
        neg_max = sb("neg_max", [P, ST])
        row_sum = sb("row_sum", [P, ST])
        rinv = sb("rinv", [P, ST])
        stats = sb("stats", [P, ST, 6])
        moments = sb("moments", [P, 6, ST])
        rstd = sb("rstd", [P, 4, ST])
        gate = sb("gate", [P, 6, E])
        thr = sb("thr", [P, 10])
        zero = sb("zero", [P, 1])
        neg_bthr = sb("neg_bthr", [P, 1])
        bthr_wide = sb("bthr_wide", [P, 1])

        def prob_tile(i):
            if i < TC:
                return prob[:, i * CH:(i + 1) * CH]
            at = TC * CH + (i - TC) * S
            return prob[:, at:at + S]

        ffn = ctxT[:, :, :, :].rearrange("p a r s -> p (a r s)")
        wb_parts = ffn[:, 0:2 * KT * HID].rearrange("p (a k n) -> p a k n", a=2, k=KT)
        at = 2 * KT * HID
        wg_parts = ffn[:, at:at + 2 * KT * NGATE].rearrange("p (a k n) -> p a k n", a=2, k=KT)
        at += 2 * KT * NGATE
        ba_parts = ffn[:, at:at + 2 * HID].rearrange("p (a n) -> p a n", a=2)
        gated_parts = v[:, :, 0, :]
        wb_raw = prob[:, 0:KT * HID].rearrange("p (k n) -> p k n", k=KT)
        at = KT * HID
        wg_raw = prob[:, at:at + KT * NGATE].rearrange("p (k n) -> p k n", k=KT)
        at += KT * NGATE
        ba_raw = prob[:, at:at + HID]
        at += HID
        bias_sum = prob[:, at:at + HID]
        bias_o = prob[:, at + HID:at + 2 * HID]
        at += 2 * HID
        xn = prob[:, at:at + 2 * HID].rearrange("p (a n) -> p a n", a=2)
        gated = vT[:, 0:2 * P].rearrange("p (a n) -> p a n", a=2)

        scores = ctx.enter_context(nc.psum_tensor("scores", [P, 4, CH], f32))
        turned = ctx.enter_context(nc.psum_tensor("turned", [P, LAG, CH], f32))
        attended = ctx.enter_context(nc.psum_tensor("attended", [P, CH], f32))
        shared = ctx.enter_context(nc.psum_tensor("shared", [P, CH], f32))

        def score_bank(i):
            if i < TC:
                return scores[:, i, :]
            b = 2 * (i % 2)
            return scores[:, b:b + 2, :].rearrange("p b n -> p (b n)")

        const_in = sem("const_in")
        const_ok = sem("const_ok")
        zero_ok = sem("zero_ok")
        x_in = [sem(f"x_in{i}") for i in range(2)]
        ffn_in = sem("ffn_in")
        ffn_split = sem("ffn_split")
        bias_ok = sem("bias_ok")
        bias_added = sem("bias_added")
        var_ready = sem("var_ready")
        rstd_ready = sem("rstd_ready")
        stat_step = sem("stat_step")
        sqrt_done = sem("sqrt_done")
        xn_ready = sem("xn_ready")
        x_turned = sem("x_turned")
        x_hi = sem("x_hi")
        x_lo = sem("x_lo")
        base_done = sem("base_done")
        gate_done = sem("gate_done")
        gate_max = sem("gate_max")
        gate_exp = sem("gate_exp")
        gate_step = sem("gate_step")
        weight_step = sem("weight_step")
        gated_ready = sem("gated_ready")
        gated_turned = sem("gated_turned")
        gated_hi = sem("gated_hi")
        gated_lo = sem("gated_lo")
        moe_done = sem("moe_done")
        ffn_added = sem("ffn_added")
        wq_in, wk_in, wv_in, wo_in = sem("wq_in"), sem("wk_in"), sem("wv_in"), sem("wo_in")
        wq_split, wk_split, wv_split, wo_split = (sem("wq_split"), sem("wk_split"),
                                                  sem("wv_split"), sem("wo_split"))
        scored = sem("scored")
        max_ready = sem("max_ready")
        exp_done = sem("exp_done")
        block_turned = sem("block_turned")
        block_hi = sem("block_hi")
        block_lo = sem("block_lo")
        block_used = sem("block_used")
        rinv_ready = sem("rinv_ready")
        rinv_spread = sem("rinv_spread")
        rinv_copied = sem("rinv_copied")
        ctx_normed = sem("ctx_normed")
        ctx_hi = sem("ctx_hi")
        ctx_lo = sem("ctx_lo")
        proj_done = sem("proj_done")
        proj_biased = sem("proj_biased")
        bias_moved = sem("bias_moved")
        proj_cos = sem("proj_cos")
        proj_sin = sem("proj_sin")
        proj_rotated = sem("proj_rotated")
        proj_hi = sem("proj_hi")
        proj_lo = sem("proj_lo")
        v_done = sem("v_done")
        v_biased = sem("v_biased")
        v_turned = sem("v_turned")
        v_hi = sem("v_hi")
        v_lo = sem("v_lo")
        out_done = sem("out_done")
        out_added = sem("out_added")
        stored = sem("stored")
        batch_over = sem("batch_over")

        def tile_no(G, r, i):
            return G * (RH * ST) + (r * ST + i)

        def slot_no(G, r, s):
            return G * (RH * SLOTS) + (r * SLOTS + s)

        def chunk_no(G, r, c):
            return G * (2 * RH) + (2 * r + c)

        def head_no(G, r):
            return G * RH + r

        def unit_no(G, j):
            return G * UNITS + j

        def v_no(G, k):
            return G * 2 + k

        def out_no(G, p, t):
            return G * (2 * ST) + (p * ST + t)

        def wait_shared_bank(eng, G, unit):
            kind = unit[0]
            if kind == "rinv":
                eng.wait_ge(rinv_copied, chunk_no(G, unit[1], unit[2]) + 1)
            elif kind == "proj":
                eng.wait_ge(proj_biased, unit_no(G, unit[1]) + 1)
            elif kind == "vproj":
                eng.wait_ge(v_biased, v_no(G, unit[1]) + 1)
            elif kind == "vturn":
                eng.wait_ge(v_lo, v_no(G, unit[1]) + 1)
            else:
                eng.wait_ge(out_added, out_no(G, unit[1], unit[2]) + 1)

        def wait_batch_stored(eng, b):
            eng.wait_ge(batch_over, b + 1)

        block = ctx.enter_context(nc.Block())

        @block.sync
        def _(sp):
            sp.dma_start(cos_sin[:, :, :], tables[:, 0:2 * S].rearrange("p (a s) -> p a s", a=2))\
              .then_inc(const_in, 16)
            sp.dma_start(ident[:, :], tables[:, 2 * S:2 * S + P]).then_inc(const_in, 16)
            sp.dma_start(mask[:, :], tables[:, 2 * S + P:2 * S + 2 * P]).then_inc(const_in, 16)
            sp.dma_start(bias[:, :], bqkv).then_inc(const_in, 16)
            sp.dma_start(bthr_wide[:, :], bthr.partition_broadcast(P)).then_inc(const_in, 16)

            def load_q(g, G, r, first=False):
                if not first:
                    sp.wait_ge(wq_split, head_no(G, r) * 2)
                sp.dma_start(wq_raw[:, :, :], wq[bass.ds(g * RH + r, 1), :, :, :]
                             .rearrange("o p k d -> (o p) k d")).then_inc(wq_in, 16)

            def load_k(g, G, ahead):
                if ahead:
                    sp.wait_ge(wk_split, (G + ahead) * 2)
                sp.dma_start(wk_raw[:, :, :], wk[bass.ds(g + ahead, 1), :, :, :]
                             .rearrange("o p k d -> (o p) k d")).then_inc(wk_in, 16)

            def load_v(g, G, ahead):
                if ahead:
                    sp.wait_ge(wv_split, (G + ahead) * 2)
                sp.dma_start(wv_raw[:, :, :], wv[bass.ds(g + ahead, 1), :, :, :]
                             .rearrange("o p k d -> (o p) k d")).then_inc(wv_in, 16)

            def load_o(g, G, p, first=False):
                if not first:
                    sp.wait_ge(wo_split, (G * 2 + p) * 2)
                sp.dma_start(wo_raw[:, :, :], wo[bass.ds(g * RH + 2 * p, 2), :, :]
                             .rearrange("h d n -> d h n")).then_inc(wo_in, 16)

            with sp.Fori(0, B) as b:
                for t in range(ST):
                    sp.dma_start(acc[:, t, :], x[bass.ds(b, 1), t * P:(t + 1) * P, :]
                                 .rearrange("o p n -> (o p) n")).then_inc(x_in[t // 4], 16)
                sp.dma_start(wb_raw, wbase).then_inc(ffn_in, 16)
                sp.dma_start(wg_raw, wgate).then_inc(ffn_in, 16)
                sp.dma_start(ba_raw, badapt).then_inc(ffn_in, 16)
                sp.dma_start(bias_sum, bbase.partition_broadcast(P)).then_inc(ffn_in, 16)
                sp.dma_start(bias_o, bo.partition_broadcast(P)).then_inc(ffn_in, 16)
                G0 = b * GROUPS
                load_k(0, G0, 0)
                load_v(0, G0, 0)
                load_q(0, G0, 0, True)
                load_q(0, G0, 1)

                def load_group(g, G, first):
                    load_q(g, G, 2)
                    load_v(g, G, 1)
                    load_o(g, G, 0, first)
                    load_q(g, G, 3)
                    load_o(g, G, 1)
                    load_k(g, G, 1)
                    load_q(g, G, 4)
                    load_q(g, G, 5)

                load_group(0, G0, True)
                with sp.Fori(1, GROUPS - 1) as g:
                    load_group(g, b * GROUPS + g, False)
                last = GROUPS - 1
                load_q(last, G0 + last, 2)
                load_o(last, G0 + last, 0)
                load_q(last, G0 + last, 3)
                load_o(last, G0 + last, 1)
                for t in range(ST):
                    sp.wait_ge(out_added, b * (2 * GROUPS * ST) + ((2 * GROUPS - 1) * ST + t + 1))
                    sp.dma_start(out[bass.ds(b, 1), t * P:(t + 1) * P, :]
                                 .rearrange("o p n -> (o p) n"), acc[:, t, :]).then_inc(stored, 16)
                sp.wait_ge(stored, b * (16 * ST) + 16 * ST)
                sp.sem_inc(batch_over, 1)

        @block.gpsimd
        def _(pool):
            def split(hi, lo, raw, done, count):
                zeros = zero[:, 0:1]
                for _ in raw.shape[2:]:
                    zeros = zeros.unsqueeze(2)
                pool.tensor_tensor(hi, raw, zeros.to_broadcast(list(raw.shape)), ALU.add)\
                    .then_inc(done, 1)
                pool.wait_ge(done, count + 1)
                pool.tensor_tensor(lo, raw, hi.bitcast(f32), ALU.subtract).then_inc(done, 1)

            def split_q(G, r):
                pool.wait_ge(wq_in, (head_no(G, r) + 1) * 16)
                ahead, r4 = divmod(r, RH)
                if r:
                    pool.wait_ge(proj_done, unit_no(G, UNITS * ahead + (2 + 2 * r4 if r4 else 0)))
                split(wq_parts[:, HI, :, :], wq_parts[:, LO, :, :], wq_raw[:, :, :],
                      wq_split, head_no(G, r) * 2)

            def split_k(G, ahead):
                pool.wait_ge(wk_in, (G + (ahead + 1)) * 16)
                if ahead:
                    pool.wait_ge(proj_done, unit_no(G, 3))
                split(wk_parts[:, HI, :, :], wk_parts[:, LO, :, :], wk_raw[:, :, :],
                      wk_split, (G + ahead) * 2)

            def split_v(G, ahead):
                pool.wait_ge(wv_in, (G + (ahead + 1)) * 16)
                if ahead:
                    pool.wait_ge(v_done, v_no(G, 2))
                split(wv_parts[:, HI, :, :], wv_parts[:, LO, :, :], wv_raw[:, :, :],
                      wv_split, (G + ahead) * 2)

            def split_o(G, p, has_prev):
                pool.wait_ge(wo_in, (G * 2 + (p + 1)) * 16)
                if has_prev:
                    pool.wait_ge(out_done, out_no(G, p - 1, 0))
                split(wo_parts[:, p, HI, :, :], wo_parts[:, p, LO, :, :], wo_raw[:, :, :],
                      wo_split, (G * 2 + p) * 2)

            def rotate(G, j):
                n, a = unit_no(G, j), j % 2
                c = proj_target(j)[1]
                pool.wait_ge(proj_biased, n + 1)
                if j >= 2:
                    pool.wait_ge(proj_lo, unit_no(G, j - 1))
                pool.tensor_tensor(rotated[:, a, :], biased[:, a, :],
                                   cos_sin[:, 0, c * CH:(c + 1) * CH], ALU.mult)\
                    .then_inc(proj_cos, 1)

            def rotated_low(G, j):
                what, c, _ = proj_target(j)
                to = (qT if what == "q" else kT)[:, :, c * CH:(c + 1) * CH]
                pool.wait_ge(proj_hi, unit_no(G, j) + 1)
                pool.tensor_tensor(to[:, LO, :], rotated[:, j % 2, :], to[:, HI, :].bitcast(f32),
                                   ALU.subtract).then_inc(proj_lo, 1)

            def ctx_low(G, r, c):
                to = ctxT[:, :, r % RH, c * CH:(c + 1) * CH]
                pool.wait_ge(ctx_hi, chunk_no(G, r, c) + 1)
                pool.tensor_tensor(to[:, LO, :], normed[:, :], to[:, HI, :].bitcast(f32),
                                   ALU.subtract).then_inc(ctx_lo, 1)

            def group(G, has_prev, has_next):
                for r in range(RH):
                    for s in range(SLOTS):
                        if s == 2 and (r or has_prev):
                            ctx_low(G, r - 1, 1)
                        if s == 6:
                            ctx_low(G, r, 0)
                        for u in units_of(r, s - PART_LAG, has_prev, has_next):
                            if u[0] == "proj":
                                rotated_low(G, u[1])
                        for u in units_of(r, s, has_prev, has_next):
                            if u[0] == "proj":
                                rotate(G, u[1])
                        if s == 9 and (r < 2 or has_next):
                            split_q(G, r + 2)
                        if s == 10 and r == 0 and has_next:
                            split_v(G, 1)
                        if s == 3 and r == 1:
                            split_o(G, 0, has_prev)
                        if s == 10 and r == 2 and has_next:
                            split_k(G, 1)
                        if s == 2 and r == 2:
                            split_o(G, 1, has_prev)

            pool.memset(zero[:, :], 0.0).then_inc(zero_ok, 1)
            pool.wait_ge(zero_ok, 1)
            with pool.Fori(0, B) as b:
                pool.wait_ge(ffn_in, b * (16 * 5) + 16 * 5)
                split(wb_parts[:, HI, :, :], wb_parts[:, LO, :, :], wb_raw, ffn_split, b * 6)
                split(wg_parts[:, HI, :, :], wg_parts[:, LO, :, :], wg_raw, ffn_split, b * 6 + 2)
                split(ba_parts[:, HI, :], ba_parts[:, LO, :], ba_raw, ffn_split, b * 6 + 4)
                pool.tensor_tensor(bias_sum, bias_sum, bias_o, ALU.add).then_inc(bias_ok, 1)
                G0 = b * GROUPS
                split_k(G0, 0)
                split_q(G0, 0)
                split_v(G0, 0)
                for j in range(PRE_UNITS):
                    rotate(G0, j)
                    rotated_low(G0, j)
                split_q(G0, 1)
                group(G0, False, True)
                with pool.Fori(1, GROUPS - 1) as g:
                    group(b * GROUPS + g, True, True)
                group(G0 + (GROUPS - 1), True, False)
                ctx_low(G0 + (GROUPS - 1), RH - 1, 1)
                wait_batch_stored(pool, b)

        @block.scalar
        def _(act):
            def copy(to, source):
                return act.activation(to, source, ACT.Copy)

            def exponentials(G, r, i, first):
                n = (i + 1) * P
                c = i // TC
                act.wait_ge(max_ready, tile_no(G, r, i) + 1)
                if not first:
                    act.wait_ge(block_turned, slot_no(G, r - 1, i if c == 0 else TC + i) + 1)
                    if i % TC == 0:
                        act.wait_ge(rinv_ready, chunk_no(G, r - 1, c) + 1)
                act.activation(prob_tile(i)[:, 0:n], score_bank(i)[:, 0:n], ACT.Exp,
                               bias=neg_max[:, i:i + 1], accum_out=row_sum[:, i:i + 1])\
                   .then_inc(exp_done, 1)

            def block_high(G, r, s, first):
                a, at = s % 2, block_start(s)
                act.wait_ge(block_turned, slot_no(G, r, s) + 1)
                if not first or s >= LAG:
                    act.wait_ge(block_used, slot_no(G, r, s - LAG) + 1)
                copy(probT[:, a, HI, at:CH], turned[:, a, at:CH]).then_inc(block_hi, 1)

            def projected(G, j):
                what, _, r = proj_target(j)
                if j < PRE_UNITS:
                    column = bias[:, GROUPS * NB + (what == "k"):GROUPS * NB + 1 + (what == "k")]
                else:
                    column = bias_now[:, r - 1:r] if what == "q" else bias_now[:, RH:RH + 1]
                    act.wait_ge(bias_moved, G + 1)
                act.wait_ge(proj_done, unit_no(G, j) + 1)
                if j >= 2:
                    act.wait_ge(proj_cos, unit_no(G, j - 1))
                    act.wait_ge(proj_sin, unit_no(G, j - 1) * 2)
                act.activation(biased[:, j % 2, :], shared[:, :], ACT.Identity,
                               bias=column).then_inc(proj_biased, 1)

            def rotated_high(G, j):
                what, c, r = proj_target(j)
                to = (qT if what == "q" else kT)[:, HI, c * CH:(c + 1) * CH]
                act.wait_ge(proj_rotated, unit_no(G, j) + 1)
                if j >= PRE_UNITS:
                    i = TC - 1 if what == "q" and c == 0 else ST - 1
                    act.wait_ge(scored, tile_no(G, r - 1, i) + 1)
                copy(to, rotated[:, j % 2, :]).then_inc(proj_hi, 1)

            def v_projected(G, k):
                c = k % 2
                act.wait_ge(v_done, v_no(G, k) + 1)
                if k >= 2:
                    act.wait_ge(v_turned, v_no(G, k - 2) + 1)
                column = bias_now[:, RH + 1:RH + 2] if k >= 2 else bias[:, GROUPS * NB + 2:]
                act.activation(vT[:, c * CH:(c + 1) * CH], shared[:, :], ACT.Identity,
                               bias=column).then_inc(v_biased, 1)

            def move_bias(g):
                copy(bias_now[:, :], bias[:, bass.ds(g * NB, NB)]).then_inc(bias_moved, 1)

            def v_high(G, k, has_prev):
                u = k % 2
                act.wait_ge(v_turned, v_no(G, k) + 1)
                if k > 1 or has_prev:
                    act.wait_ge(block_used, slot_no(G, (k // 2) * RH - 1, TC + TC * u + TC - 1) + 1)
                copy(v[:, HI, TC * u:TC * (u + 1), :].rearrange("p t d -> p (t d)"),
                     shared[:, :]).then_inc(v_hi, 1)

            def rinv_copy(G, r, c, first):
                act.wait_ge(rinv_spread, chunk_no(G, r, c) + 1)
                if not first:
                    act.wait_ge(ctx_normed, chunk_no(G, r - 1, c) + 1)
                copy(rinv_wide[:, c, :], shared[:, :]).then_inc(rinv_copied, 1)

            def ctx_high(G, r, c, has_prev):
                act.wait_ge(ctx_normed, chunk_no(G, r, c) + 1)
                if c == 0 and r % 2 == 0 and has_prev:
                    act.wait_ge(out_done, out_no(G, r // 2 - 1, 0))
                copy(ctxT[:, HI, r % RH, c * CH:(c + 1) * CH], normed[:, :]).then_inc(ctx_hi, 1)

            def group(G, g, has_prev, has_next):
                for r in range(RH):
                    first = not r and not has_prev
                    for s in range(SLOTS):
                        block_high(G, r, s, first)
                        if s == 0:
                            if not first:
                                exponentials(G, r, TC, first)
                        elif score_tile(s - 1) is not None:
                            ahead, i = score_tile(s - 1)
                            if not ahead or r < RH - 1 or has_next:
                                exponentials(G, r + ahead, i, first and not ahead)
                        if s == 2 and not first:
                            ctx_high(G, r - 1, 1, has_prev)
                        if s == 6:
                            ctx_high(G, r, 0, has_prev)
                        for u in units_of(r, s, has_prev, has_next):
                            if u[0] == "rinv":
                                rinv_copy(G, r, u[2], first)
                            if u[0] == "proj":
                                projected(G, u[1])
                            if u[0] == "vproj":
                                v_projected(G, u[1])
                            if u[0] == "vturn":
                                v_high(G, u[1], has_prev)
                        for u in units_of(r, s - PART_LAG, has_prev, has_next):
                            if u[0] == "proj":
                                rotated_high(G, u[1])
                        if r == RH - 1 and s == SLOTS - 2 and has_next:
                            move_bias(g + 1)

            with act.Fori(0, B) as b:
                if True:
                    for h in range(2):
                        act.wait_ge(var_ready, b * 2 + (h + 1))
                        act.activation(rstd[:, 1, 4 * h:4 * h + 4], rstd[:, 0, 4 * h:4 * h + 4],
                                       ACT.Sqrt).then_inc(sqrt_done, 1)
                act.wait_ge(const_in, 16 * 5)
                for k in range(ST + 2):
                    T = b * ST + k
                    if k < ST:
                        act.wait_ge(x_turned, T + 1)
                        copy(xnT[:, HI, :, k * P:(k + 1) * P],
                             turned[:, k % 2, :].rearrange("p (k s) -> p k s", k=KT))\
                            .then_inc(x_hi, 1)
                    if k >= 2:
                        act.wait_ge(gated_turned, T - 1)
                        if k > 2:
                            act.wait_ge(moe_done, T - 2)
                        copy(gated_parts[:, HI, :], shared[:, 0:P]).then_inc(gated_hi, 1)
                    if 1 <= k <= ST:
                        bank = scores[:, 2 + (k - 1) % 2, :]
                        act.wait_ge(gate_max, T)
                        act.activation(gate[:, 0, :], bank[:, E * R:E * R + E], ACT.Exp,
                                       bias=thr[:, 0:1], accum_out=thr[:, 1:2])\
                           .then_inc(gate_exp, 1)
                        act.activation(thr[:, 2:3], bank[:, E * R + E:E * R + E + 1], ACT.Exp,
                                       bias=neg_bthr[:, 0:1], scale=-1.0).then_inc(gate_exp, 1)
                G0 = b * GROUPS
                projected(G0, 0)
                projected(G0, 1)
                rotated_high(G0, 0)
                projected(G0, 2)
                rotated_high(G0, 1)
                projected(G0, 3)
                rotated_high(G0, 2)
                v_projected(G0, 0)
                v_projected(G0, 1)
                rotated_high(G0, 3)
                v_high(G0, 0, False)
                move_bias(0)
                for i in range(TC + 1):
                    exponentials(G0, 0, i, True)
                group(G0, 0, False, True)
                with act.Fori(1, GROUPS - 1) as g:
                    group(b * GROUPS + g, g, True, True)
                group(G0 + (GROUPS - 1), GROUPS - 1, True, False)
                ctx_high(G0 + (GROUPS - 1), RH - 1, 1, True)
                wait_batch_stored(act, b)

        @block.vector
        def _(dve):
            def row_max(G, r, i):
                dve.wait_ge(scored, tile_no(G, r, i) + 1)
                dve.reduce_max(neg_max[:, i:i + 1], score_bank(i)[:, 0:(i + 1) * P], AX.X,
                               negate=True).then_inc(max_ready, 1)

            def inverse(G, r, c, first):
                dve.wait_ge(exp_done, tile_no(G, r, TC * c + TC - 1) + 1)
                if not first:
                    dve.wait_ge(rinv_spread, chunk_no(G, r - 1, c) + 1)
                dve.reciprocal(rinv[:, TC * c:TC * c + TC], row_sum[:, TC * c:TC * c + TC])\
                   .then_inc(rinv_ready, 1)

            def block_low(G, r, s):
                a, at = s % 2, block_start(s)
                dve.wait_ge(block_hi, slot_no(G, r, s) + 1)
                dve.tensor_tensor(probT[:, a, LO, at:CH], turned[:, a, at:CH],
                                  probT[:, a, HI, at:CH].bitcast(f32), ALU.subtract)\
                   .then_inc(block_lo, 1)

            def cross(G, j):
                n, a = unit_no(G, j), j % 2
                c = proj_target(j)[1]
                half = D // 2
                dve.wait_ge(proj_biased, n + 1)
                if j >= 2:
                    dve.wait_ge(proj_rotated, unit_no(G, j - 1))
                for to, of in ((0, half), (half, 0)):
                    dve.tensor_tensor(crossed[to:to + half, a, :], biased[of:of + half, a, :],
                                      cos_sin[of:of + half, 1, c * CH:(c + 1) * CH], ALU.mult)\
                       .then_inc(proj_sin, 1)

            def rotate(G, j):
                n, a = unit_no(G, j), j % 2
                dve.wait_ge(proj_cos, n + 1)
                dve.wait_ge(proj_sin, n * 2 + 2)
                dve.tensor_tensor(rotated[:, a, :], rotated[:, a, :], crossed[:, a, :], ALU.add)\
                   .then_inc(proj_rotated, 1)

            def v_low(G, k):
                u = k % 2
                dve.wait_ge(v_hi, v_no(G, k) + 1)
                to = v[:, :, TC * u:TC * (u + 1), :].rearrange("p a t d -> p a (t d)")
                dve.tensor_tensor(to[:, LO, :], shared[:, :], to[:, HI, :].bitcast(f32),
                                  ALU.subtract).then_inc(v_lo, 1)

            def normalise(G, r, c, first=False):
                n = chunk_no(G, r, c)
                dve.wait_ge(block_used, slot_no(G, r, TC - 1 if c == 0 else SLOTS - 1) + 1)
                dve.wait_ge(rinv_copied, n + 1)
                if not first:
                    dve.wait_ge(ctx_lo, n)
                dve.tensor_tensor(normed[:, :], attended[:, :], rinv_wide[:, c, :], ALU.mult)\
                   .then_inc(ctx_normed, 1)

            def add_out(G, p, t):
                dve.wait_ge(out_done, out_no(G, p, t) + 1)
                dve.wait_ge(out_added, out_no(G, p - 1, t) + 1)
                dve.tensor_tensor(acc[:, t, :], acc[:, t, :], shared[:, :], ALU.add)\
                   .then_inc(out_added, 1)

            def add_out_first(G, t):
                dve.wait_ge(out_done, out_no(G, 0, t) + 1)
                dve.tensor_tensor(acc[:, t, :], acc[:, t, :], shared[:, :], ALU.add)\
                   .then_inc(out_added, 1)

            def group(G, has_prev, has_next):
                for r in range(RH):
                    first = not r and not has_prev
                    for s in range(SLOTS):
                        if s in (0, 4):
                            inverse(G, r, s // TC, first)
                        if s == 1 and not first:
                            normalise(G, r - 1, 1)
                        if s == 5:
                            normalise(G, r, 0, first)
                        block_low(G, r, s)
                        for u in units_of(r, s - 2, has_prev, has_next):
                            if u[0] == "proj":
                                rotate(G, u[1])
                        if score_tile(s) is not None:
                            ahead, i = score_tile(s)
                            if not ahead or r < RH - 1 or has_next:
                                row_max(G, r + ahead, i)
                        for u in units_of(r, s - 1, has_prev, has_next):
                            if u[0] == "proj":
                                cross(G, u[1])
                        for u in units_of(r, s, has_prev, has_next):
                            if u[0] == "vturn":
                                v_low(G, u[1])
                            if u[0] == "out":
                                if has_prev:
                                    add_out(G, u[1], u[2])
                                else:
                                    add_out_first(G, u[2])

            dve.wait_ge(const_in, 16 * 5)
            dve.tensor_copy(ident_b[:, :], ident[:, :]).then_inc(const_ok, 1)
            dve.tensor_copy(mask_b[:, :], mask[:, :]).then_inc(const_ok, 1)
            dve.tensor_scalar(neg_bthr[:, 0:1], bthr_wide[:, :], -1.0, None, ALU.mult)\
               .then_inc(const_ok, 1)
            with dve.Fori(0, B) as b:
                def chained(instruction, done, count):
                    instruction.then_inc(done, 1)
                    dve.wait_ge(done, count)

                for h in range(2):
                    four = slice(4 * h, 4 * h + 4)
                    dve.wait_ge(x_in[h], b * 64 + 64)
                    for t in range(4 * h, 4 * h + 4):
                        last = dve.bn_stats(stats[:, t, :], acc[:, t, :])
                    chained(last, stat_step, b * 14 + (7 * h + 1))
                    even, odd = stats[:, four, 0:3], stats[:, four, 3:6]
                    dve.tensor_tensor(moments[:, 0, four], even[:, :, 1], odd[:, :, 1], ALU.add)
                    dve.tensor_tensor(moments[:, 1, four], even[:, :, 1], odd[:, :, 1],
                                      ALU.subtract)
                    chained(dve.tensor_tensor(moments[:, 2, four], even[:, :, 2], odd[:, :, 2],
                                              ALU.add), stat_step, b * 14 + (7 * h + 2))
                    dve.tensor_scalar(moments[:, 3, four], moments[:, 0, four], 0.5, None,
                                      ALU.mult)
                    dve.tensor_tensor(moments[:, 4, four], moments[:, 1, four],
                                      moments[:, 1, four], ALU.mult)
                    chained(dve.tensor_scalar(moments[:, 5, four], moments[:, 2, four],
                                              1.0 / HID, EPS, ALU.mult, ALU.add),
                            stat_step, b * 14 + (7 * h + 3))
                    chained(dve.scalar_tensor_tensor(rstd[:, 0, four], moments[:, 4, four], 0.25,
                                                     moments[:, 5, four], ALU.mult, ALU.add),
                            var_ready, b * 2 + (h + 1))
                    dve.wait_ge(sqrt_done, b * 2 + (h + 1))
                    chained(dve.reciprocal(rstd[:, 2, four], rstd[:, 1, four]),
                            stat_step, b * 14 + (7 * h + 4))
                    chained(dve.tensor_tensor(rstd[:, 3, four], rstd[:, 2, four],
                                              rstd[:, 2, four], ALU.mult),
                            stat_step, b * 14 + (7 * h + 5))
                    chained(dve.tensor_tensor(rstd[:, 3, four], rstd[:, 3, four],
                                              rstd[:, 0, four], ALU.mult),
                            stat_step, b * 14 + (7 * h + 6))
                    chained(dve.tensor_scalar(rstd[:, 3, four], rstd[:, 3, four], -0.5, 1.5,
                                              ALU.mult, ALU.add),
                            stat_step, b * 14 + (7 * h + 7))
                    chained(dve.tensor_tensor(rstd[:, 2, four], rstd[:, 2, four],
                                              rstd[:, 3, four], ALU.mult),
                            rstd_ready, b * 2 + (h + 1))

                def normalised(t):
                    T = b * ST + t
                    if t >= 2:
                        dve.wait_ge(x_turned, T - 1)
                    dve.tensor_scalar(xn[:, t % 2, :], acc[:, t, :], moments[:, 3, t:t + 1],
                                      rstd[:, 2, t:t + 1], ALU.subtract, ALU.mult)\
                       .then_inc(xn_ready, 1)

                def gating(t):
                    T = b * ST + t
                    bank = scores[:, 2 + t % 2, :]

                    def step(instruction, k):
                        chained(instruction, gate_step, T * 7 + k)
                    dve.wait_ge(gate_done, T + 1)
                    dve.reduce_max(thr[:, 0:1], bank[:, E * R:E * R + E], AX.X, negate=True)\
                       .then_inc(gate_max, 1)
                    dve.wait_ge(gate_exp, T * 2 + 2)
                    dve.reciprocal(thr[:, 3:4], thr[:, 1:2])
                    step(dve.tensor_scalar(thr[:, 4:5], thr[:, 2:3], 1.0, None, ALU.add), 1)
                    step(dve.reciprocal(thr[:, 5:6], thr[:, 4:5]), 2)
                    step(dve.tensor_scalar(thr[:, 6:7], thr[:, 5:6], MAX_THR, None, ALU.mult), 3)
                    step(dve.tensor_scalar(gate[:, 1, :], gate[:, 0, :], thr[:, 3:4], thr[:, 6:7],
                                           ALU.mult, ALU.subtract), 4)
                    step(dve.tensor_scalar(gate[:, 2, :], gate[:, 1, :], 0.0, None, ALU.max), 5)
                    step(dve.reduce_sum(thr[:, 7:8], gate[:, 2, :], AX.X), 6)
                    step(dve.scalar_tensor_tensor(thr[:, 8:9], thr[:, 7:8], 0.0, thr[:, 7:8],
                                                  ALU.is_equal, ALU.add), 7)
                    chained(dve.reciprocal(thr[:, 9:10], thr[:, 8:9]), weight_step, T * 2 + 1)
                    chained(dve.tensor_scalar(gate[:, 3, :], gate[:, 2, :], thr[:, 9:10], SCALING,
                                              ALU.mult, ALU.mult), weight_step, T * 2 + 2)
                    if t >= 2:
                        dve.wait_ge(gated_turned, T - 1)
                    dve.tensor_tensor(gated[:, t % 2, :].rearrange("p (e r) -> p e r", e=E),
                                      bank[:, 0:E * R].rearrange("p (e r) -> p e r", e=E),
                                      gate[:, 3, :].unsqueeze(2).to_broadcast([P, E, R]),
                                      ALU.mult).then_inc(gated_ready, 1)

                dve.wait_ge(bias_ok, b + 1)
                normalised(0)
                for k in range(ST + 2):
                    T = b * ST + k
                    if k + 1 < ST:
                        normalised(k + 1)
                    if k < ST:
                        dve.wait_ge(x_hi, T + 1)
                        part = xnT[:, :, :, k * P:(k + 1) * P]
                        dve.tensor_tensor(part[:, LO, :, :],
                                          turned[:, k % 2, :].rearrange("p (k s) -> p k s", k=KT),
                                          part[:, HI, :, :].bitcast(f32), ALU.subtract)\
                           .then_inc(x_lo, 1)
                    if k >= 2:
                        dve.wait_ge(gated_hi, T - 1)
                        dve.tensor_tensor(gated_parts[:, LO, :], shared[:, 0:P],
                                          gated_parts[:, HI, :].bitcast(f32), ALU.subtract)\
                           .then_inc(gated_lo, 1)
                    if 1 <= k <= ST:
                        gating(k - 1)
                    if k >= 2:
                        t = k - 2
                        dve.wait_ge(xn_ready, T - 1)
                        dve.tensor_tensor(acc[:, t, :], acc[:, t, :], bias_sum, ALU.add)\
                           .then_inc(bias_added, 1)
                        dve.wait_ge(moe_done, T - 1)
                        dve.wait_ge(bias_added, T - 1)
                        dve.tensor_tensor(acc[:, t, :], acc[:, t, :], scores[:, t % 2, :], ALU.add)\
                           .then_inc(ffn_added, 1)
                G0 = b * GROUPS
                for j in range(PRE_UNITS):
                    cross(G0, j)
                    rotate(G0, j)
                v_low(G0, 0)
                for i in range(TC + 1):
                    row_max(G0, 0, i)
                dve.wait_ge(ffn_added, b * ST + ST)
                group(G0, False, True)
                with dve.Fori(1, GROUPS - 1) as g:
                    group(b * GROUPS + g, True, True)
                last = G0 + (GROUPS - 1)
                group(last, True, False)
                normalise(last, RH - 1, 1)
                for t in range(ST):
                    add_out(last, 1, t)
                wait_batch_stored(dve, b)

        @block.tensor
        def _(pe):
            def product(to, lhs, rhs, first=True, last=True):
                for n, (a, c) in enumerate(((HI, HI), (HI, LO), (LO, HI))):
                    mm = pe.matmul(to, lhs[a], rhs[c], start=first and n == 0,
                                   stop=last and n == 2)
                return mm

            def parts(t, *at):
                return t[(slice(None), HI, *at)], t[(slice(None), LO, *at)]

            def score(G, r, i, first):
                c = i // TC
                if i % TC == 0:
                    ahead, r4 = divmod(r, RH)
                    j = UNITS * ahead + (1 + 2 * c if r4 == 0 else 2 + 2 * r4 + c)
                    pe.wait_ge(proj_lo, unit_no(G, j) + 1)
                if c == 0 and not first:
                    pe.wait_ge(exp_done, tile_no(G, r - 1, 6 + i // 2) + 1)
                if c == 1:
                    pe.wait_ge(exp_done, tile_no(G, r, (1, 3, 4, 5)[i - TC]) + 1)
                bank = score_bank(i)
                q = parts(qT, slice(i * P, (i + 1) * P))
                n = (i + 1) * P
                for at in range(0, n, CH):
                    to = min(at + CH, n)
                    diagonal = to == n
                    mm = product(bank[:, at:to], q, parts(kT, slice(at, to)), last=not diagonal)
                    if diagonal:
                        mm = pe.matmul(bank[:, n - P:n], ident_b[:, :], mask_b[:, :],
                                       start=False, stop=True)
                mm.then_inc(scored, 1)

            def turn_block(G, r, s, first):
                c, j = chunk_block(s)
                if s in (0, TC):
                    pe.wait_ge(exp_done, tile_no(G, r, TC * c + TC - 1) + 1)
                if not first or s >= LAG:
                    pe.wait_ge(block_lo, slot_no(G, r, s - LAG) + 1)
                for i in range(block_start(s) // P, TC):
                    mm = pe.matmul(turned[:, s % 2, i * P:(i + 1) * P],
                                   prob_tile(TC * c + i)[:, j * P:(j + 1) * P], ident[:, :],
                                   is_transpose=True)
                mm.then_inc(block_turned, 1)

            def attend(G, r, s, first):
                c, j = chunk_block(s)
                if j == 0 and not (first and c == 0):
                    pe.wait_ge(ctx_normed, chunk_no(G, r, c))
                if r == 0 and s in (0, TC + TC):
                    pe.wait_ge(v_lo, v_no(G, s // (2 * TC)) + 1)
                pe.wait_ge(block_lo, slot_no(G, r, s) + 1)
                at = block_start(s)
                product(attended[:, at:CH], parts(v, j),
                        (probT[:, s % 2, HI, at:CH], probT[:, s % 2, LO, at:CH]),
                        first=j == 0, last=j == TC * c + TC - 1).then_inc(block_used, 1)

            def project(G, j):
                what, c, r = proj_target(j)
                if what == "q":
                    pe.wait_ge(wq_split, head_no(G, r) * 2 + 2)
                    w = wq_parts
                else:
                    pe.wait_ge(wk_split, (G + r // RH) * 2 + 2)
                    w = wk_parts
                for k in range(KT):
                    mm = product(shared[:, :], parts(w, k),
                                 parts(xnT, k, slice(c * CH, (c + 1) * CH)),
                                 first=k == 0, last=k == KT - 1)
                mm.then_inc(proj_done, 1)

            def project_v(G, k):
                c = k % 2
                pe.wait_ge(wv_split, (G + k // 2) * 2 + 2)
                for b in range(KT):
                    mm = product(shared[:, :], parts(wv_parts, b),
                                 parts(xnT, b, slice(c * CH, (c + 1) * CH)),
                                 first=b == 0, last=b == KT - 1)
                mm.then_inc(v_done, 1)

            def turn_v(G, k):
                u = k % 2
                pe.wait_ge(v_biased, v_no(G, k) + 1)
                for i in range(TC):
                    mm = pe.matmul(shared[:, i * P:(i + 1) * P],
                                   vT[:, (TC * u + i) * P:(TC * u + i + 1) * P], ident[:, :],
                                   is_transpose=True)
                mm.then_inc(v_turned, 1)

            def spread_rinv(G, r, c):
                pe.wait_ge(rinv_ready, chunk_no(G, r, c) + 1)
                for i in range(TC):
                    mm = pe.matmul(shared[:, i * P:(i + 1) * P],
                                   rinv[:, TC * c + i:TC * c + i + 1].to_broadcast([P, P]),
                                   ident[:, :], is_transpose=True)
                mm.then_inc(rinv_spread, 1)

            def project_out(G, p, t):
                pe.wait_ge(ctx_lo, chunk_no(G, 2 * p + 1, t // TC) + 1)
                pe.wait_ge(wo_split, G * 4 + (2 * p + 2))
                for h in range(2):
                    r = (2 * p + h) % RH
                    mm = product(shared[:, :], parts(ctxT, r, slice(t * P, (t + 1) * P)),
                                 (wo_parts[:, p % 2, HI, h, :], wo_parts[:, p % 2, LO, h, :]),
                                 first=h == 0, last=h == 1)
                mm.then_inc(out_done, 1)

            def unit(G, u):
                if u[0] == "rinv":
                    spread_rinv(G, u[1], u[2])
                elif u[0] == "proj":
                    project(G, u[1])
                elif u[0] == "vproj":
                    project_v(G, u[1])
                elif u[0] == "vturn":
                    turn_v(G, u[1])
                else:
                    project_out(G, u[1], u[2])

            def group(G, has_prev, has_next):
                previous = ("rinv", -1, 1) if has_prev else ("vturn", 0)
                for r in range(RH):
                    first = not r and not has_prev
                    for s in range(SLOTS):
                        turn_block(G, r, s, first)
                        if s == 2:
                            score(G, r, TC + 3, False)
                        if s >= LAG:
                            attend(G, r, s - LAG, first)
                        elif not first:
                            attend(G, r - 1, s - LAG + SLOTS, False)
                        if score_tile(s) is not None and s != 2:
                            ahead, i = score_tile(s)
                            if not ahead or r < RH - 1 or has_next:
                                score(G, r + ahead, i, False)
                        for u in units_of(r, s, has_prev, has_next):
                            wait_shared_bank(pe, G, previous)
                            unit(G, u)
                            previous = u
                return previous

            pe.wait_ge(const_ok, 3)
            with pe.Fori(0, B) as b:
                for k in range(ST + 2):
                    T = b * ST + k
                    if k < ST:
                        pe.wait_ge(xn_ready, T + 1)
                        if k >= 2:
                            pe.wait_ge(x_lo, T - 1)
                        for i in range(KT):
                            mm = pe.matmul(turned[:, k % 2, i * P:(i + 1) * P],
                                           xn[:, k % 2, i * P:(i + 1) * P], ident[:, :],
                                           is_transpose=True)
                        mm.then_inc(x_turned, 1)
                    if k >= 2:
                        pe.wait_ge(gated_ready, T - 1)
                        if k > 2:
                            pe.wait_ge(gated_lo, T - 2)
                        pe.matmul(shared[:, 0:P], gated[:, k % 2, :], ident[:, :],
                                  is_transpose=True).then_inc(gated_turned, 1)
                    if 1 <= k <= ST:
                        t = k - 1
                        if t == 0:
                            pe.wait_ge(ffn_split, b * 6 + 6)
                        pe.wait_ge(x_lo, T)
                        tile = slice(t * P, (t + 1) * P)
                        if t >= 2:
                            pe.wait_ge(gated_ready, T - 2)
                        for i in range(KT):
                            mm = product(scores[:, 2 + t % 2, 0:NGATE], parts(xnT, i, tile),
                                         (wg_parts[:, HI, i, :], wg_parts[:, LO, i, :]),
                                         first=i == 0, last=i == KT - 1)
                        mm.then_inc(gate_done, 1)
                        if t >= 2:
                            pe.wait_ge(ffn_added, T - 2)
                        for i in range(KT):
                            product(scores[:, t % 2, :], parts(xnT, i, tile),
                                    (wb_parts[:, HI, i, :], wb_parts[:, LO, i, :]),
                                    first=i == 0, last=False)
                    if k >= 2:
                        pe.wait_ge(gated_lo, T - 1)
                        product(scores[:, k % 2, :],
                                (gated_parts[:, HI, :], gated_parts[:, LO, :]),
                                (ba_parts[:, HI, :], ba_parts[:, LO, :]),
                                first=False).then_inc(moe_done, 1)
                G0 = b * GROUPS
                for j in range(PRE_UNITS):
                    if j:
                        wait_shared_bank(pe, G0, ("proj", j - 1))
                    project(G0, j)
                wait_shared_bank(pe, G0, ("proj", PRE_UNITS - 1))
                project_v(G0, 0)
                wait_shared_bank(pe, G0, ("vproj", 0))
                project_v(G0, 1)
                wait_shared_bank(pe, G0, ("vproj", 1))
                turn_v(G0, 0)
                pe.wait_ge(ffn_added, b * ST + ST)
                for i in range(TC + 1):
                    score(G0, 0, i, True)
                group(G0, False, True)
                with pe.Fori(1, GROUPS - 1) as g:
                    group(b * GROUPS + g, True, True)
                last = G0 + (GROUPS - 1)
                previous = group(last, True, False)
                for s in (SLOTS - 2, SLOTS - 1):
                    attend(last, RH - 1, s, False)
                for t in range(ST):
                    wait_shared_bank(pe, last, previous)
                    previous = ("out", 1, t)
                    project_out(last, 1, t)
                wait_batch_stored(pe, b)


def position_tables():
    import numpy as np

    half = D // 2
    inv_freq = (1.0 / np.power(np.float32(10000.0),
                               np.arange(half, dtype=np.float32) / np.float32(half))).astype(np.float32)
    angle = (np.arange(S, dtype=np.float32)[None, :] * inv_freq[:, None]).astype(np.float32)
    scale = float(D) ** -0.25
    cos = np.cos(angle.astype(np.float64)) * scale
    sin = np.sin(angle.astype(np.float64)) * scale
    tables = np.zeros((P, 2 * S + 2 * P), np.float32)
    tables[:half, 0:S] = tables[half:, 0:S] = cos
    tables[:half, S:2 * S] = sin
    tables[half:, S:2 * S] = -sin
    tables[:, 2 * S:2 * S + P] = np.eye(P)
    tables[:, 2 * S + P:] = np.where(np.tril(np.ones((P, P), bool)), 0.0, -1e30)
    return tables


def kernel(**inputs):
    import numpy as np
    import concourse.bacc as bacc
    from concourse.bass_utils import run_bass_kernel_spmd

    a = {n: np.asarray(v) for n, v in inputs.items()}

    def by_rows(w, n):
        return w.reshape(KT, P, n, D).transpose(2, 1, 0, 3)

    gate_cols = np.concatenate([a["L0_ffn_A"].reshape(E * R, HID), a["L0_ffn_W_gate"],
                                a["L0_ffn_W_thr"], np.zeros((1, HID), np.float32)]).T
    bq, bk, bv = (a[f"L0_attn_b{n}"].reshape(-1, D) for n in "qkv")
    bias_rows = []
    for g in range(GROUPS):
        n = (g + 1) % GROUPS
        bias_rows += [bq[g * RH + 1], bq[g * RH + 2], bq[g * RH + 3], bq[n * RH], bk[n], bv[n]]
    bias_rows += [bq[0], bk[0], bv[0]]
    arrays = {
        "in_x": a["L0_attn_hidden_states"],
        "in_wq": by_rows(a["L0_attn_Wq"], H),
        "in_wk": by_rows(a["L0_attn_Wk"], GROUPS),
        "in_wv": by_rows(a["L0_attn_Wv"], GROUPS),
        "in_wo": a["L0_attn_Wo"].reshape(H, D, HID),
        "in_bqkv": np.stack(bias_rows).T,
        "in_bo": a["L0_attn_bo"],
        "in_wbase": a["L0_ffn_W_base"].T.reshape(KT, P, HID).transpose(1, 0, 2),
        "in_bbase": a["L0_ffn_b_base"],
        "in_wgate": gate_cols.reshape(KT, P, NGATE).transpose(1, 0, 2),
        "in_bthr": a["L0_ffn_b_thr"],
        "in_badapt": a["L0_ffn_B"].transpose(0, 2, 1).reshape(E * R, HID),
        "in_tables": position_tables(),
    }
    arrays = {n: np.ascontiguousarray(v) for n, v in arrays.items()}
    nc = bacc.Bacc("TRN2", target_bir_lowering=False, num_devices=1)
    f32 = mybir.dt.float32
    args = [nc.dram_tensor(n, v.shape, f32, kind="ExternalInput").ap() for n, v in arrays.items()]
    args.append(nc.dram_tensor("out", (B, S, HID), f32, kind="ExternalOutput").ap())
    build(nc, *args)
    return run_bass_kernel_spmd(nc, [arrays], core_ids=[0]).results[0]["out"]
```

```python
import concourse.bass as bass
from concourse import mybir
from contextlib import ExitStack

B, S, HID = 2, 1024, 512
H, GROUPS, D = 32, 8, 128
RH = H // GROUPS
E, R = 8, 16
P = 128
KT = HID // P
ST = S // P
CH = 512
TC = CH // P
SLOTS = TC + ST
LAG = 2
PART_LAG = 2
PROJ_SLOTS = ((2, 5), (1, 3), (2, 5), (0, 1, 3, 5))
OUT_SLOTS = ((1, 3, 8, 9, 10, 11), (9, 11), (1, 3, 8, 9, 10, 11), (7, 9))
LAST_OUT_SLOTS = (2, 4, 8, 9, 10, 11)
NGATE = E * R + E + 2
NB = RH + 2
EPS = 1e-5
MAX_THR = 1.0 / 8.0
SCALING = 2.0
UNITS = 2 * RH + 2
PRE_UNITS = 4


def chunk_block(s):
    return (0, s) if s < TC else (1, s - TC)


def block_start(s):
    c, j = chunk_block(s)
    return max(j - TC * c, 0) * P


def score_tile(s):
    if s < 3:
        return False, TC + 1 + s
    if 7 <= s < 11:
        return True, s - 7
    if s == 11:
        return True, TC
    return None


def units_of(r, s, has_prev, has_next):
    found = []
    if r == 0 and s == 6:
        found.append(("vturn", 1))
    if (r < RH - 1 or has_next) and s in PROJ_SLOTS[r]:
        found.append(("proj", PRE_UNITS + 2 * r + PROJ_SLOTS[r].index(s)))
    if r == 1 and has_next and s in (5, 7):
        found.append(("vproj", 2 + s // 7))
    if r == RH - 1 and has_next and s == 10:
        found.append(("vturn", 2))
    if r >= 2 or has_prev:
        slots = OUT_SLOTS[r]
        if r == RH - 1 and not has_next:
            if s in LAST_OUT_SLOTS:
                n = LAST_OUT_SLOTS.index(s)
                found.append(("out", 0, ST - 2 + n) if n < 2 else ("out", 1, n - 2))
        elif s in slots:
            found.append(("out", 0 if r >= 2 else -1,
                          (len(OUT_SLOTS[r - 1]) if r % 2 else 0) + slots.index(s)))
    return found


def proj_target(j):
    ahead, j = divmod(j, UNITS)
    if j < PRE_UNITS:
        return ("k", "q")[j % 2], j // 2, ahead * RH
    return "q", j % 2, (j - PRE_UNITS) // 2 + 1 + ahead * RH


def build(nc, x, wq, wk, wv, wo, bqkv, bo, wbase, bbase, wgate, bthr, badapt, tables, rinv_row, out):
    f32, f32r, bf16 = mybir.dt.float32, mybir.dt.float32r, mybir.dt.bfloat16
    ALU = mybir.AluOpType
    ACT = mybir.ActivationFunctionType
    AX = mybir.AxisListType
    ctx = ExitStack()
    with ctx:
        def sb(name, shape, dt=f32):
            return ctx.enter_context(nc.sbuf_tensor(name, shape, dt))

        def sem(name):
            return ctx.enter_context(nc.semaphore(name))

        HI, LO = 0, 1
        xnT = sb("xnT", [P, 2, KT, S], f32r)
        kT = sb("kT", [P, 2, S], f32r)
        qT = sb("qT", [P, 2, S], f32r)
        v = sb("v", [P, 2, ST, D], f32r)
        ctxT = sb("ctxT", [P, 2, RH, S], f32r)
        acc = sb("acc", [P, ST, HID])
        prob = sb("prob", [P, TC * CH + TC * S])
        probT = sb("probT", [P, LAG, 2, CH], f32r)
        wo_parts = sb("wo_parts", [P, 2, 2, 2, HID], f32r)
        wq_parts = sb("wq_parts", [P, 2, KT, D], f32r)
        wk_parts = sb("wk_parts", [P, 2, KT, D], f32r)
        wv_parts = sb("wv_parts", [P, 2, KT, D], f32r)
        wq_raw = sb("wq_raw", [P, KT, D])
        wk_raw = sb("wk_raw", [P, KT, D])
        wv_raw = sb("wv_raw", [P, KT, D])
        wo_raw = sb("wo_raw", [P, 2, HID])
        biased = sb("biased", [P, 2, CH])
        rotated = sb("rotated", [P, 2, CH])
        crossed = sb("crossed", [P, 2, CH])
        vT = sb("vT", [P, S])
        rinv_wide = sb("rinv_wide", [P, 2, CH])
        normed = sb("normed", [P, CH])
        cos_sin = sb("cos_sin", [P, 2, S])
        ident = sb("ident", [P, P])
        ident_b = sb("ident_b", [P, P], bf16)
        mask = sb("mask", [P, P])
        mask_b = sb("mask_b", [P, P], bf16)
        bias = sb("bias", [P, GROUPS * NB + 3])
        bias_now = sb("bias_now", [P, NB])
        neg_max = sb("neg_max", [P, ST])
        row_sum = sb("row_sum", [P, ST])
        rinv = sb("rinv", [P, ST])
        stats = sb("stats", [P, ST, 6])
        moments = sb("moments", [P, 6, ST])
        rstd = sb("rstd", [P, 4, ST])
        gate = sb("gate", [P, 6, E])
        thr = sb("thr", [P, 10])
        zero = sb("zero", [P, 1])
        neg_bthr = sb("neg_bthr", [P, 1])
        bthr_wide = sb("bthr_wide", [P, 1])

        def prob_tile(i):
            if i < TC:
                return prob[:, i * CH:(i + 1) * CH]
            at = TC * CH + (i - TC) * S
            return prob[:, at:at + S]

        ffn = ctxT[:, :, :, :].rearrange("p a r s -> p (a r s)")
        wb_parts = ffn[:, 0:2 * KT * HID].rearrange("p (a k n) -> p a k n", a=2, k=KT)
        at = 2 * KT * HID
        wg_parts = ffn[:, at:at + 2 * KT * NGATE].rearrange("p (a k n) -> p a k n", a=2, k=KT)
        at += 2 * KT * NGATE
        ba_parts = ffn[:, at:at + 2 * HID].rearrange("p (a n) -> p a n", a=2)
        gated_parts = v[:, :, 0, :]
        wb_raw = prob[:, 0:KT * HID].rearrange("p (k n) -> p k n", k=KT)
        at = KT * HID
        wg_raw = prob[:, at:at + KT * NGATE].rearrange("p (k n) -> p k n", k=KT)
        at += KT * NGATE
        ba_raw = prob[:, at:at + HID]
        at += HID
        bias_sum = prob[:, at:at + HID]
        bias_o = prob[:, at + HID:at + 2 * HID]
        at += 2 * HID
        xn = prob[:, at:at + 2 * HID].rearrange("p (a n) -> p a n", a=2)
        gated = vT[:, 0:2 * P].rearrange("p (a n) -> p a n", a=2)

        scores = ctx.enter_context(nc.psum_tensor("scores", [P, 4, CH], f32))
        turned = ctx.enter_context(nc.psum_tensor("turned", [P, LAG, CH], f32))
        attended = ctx.enter_context(nc.psum_tensor("attended", [P, CH], f32))
        shared = ctx.enter_context(nc.psum_tensor("shared", [P, CH], f32))

        def score_bank(i):
            if i < TC:
                return scores[:, i, :]
            b = 2 * (i % 2)
            return scores[:, b:b + 2, :].rearrange("p b n -> p (b n)")

        def unit_bank(kind, n):
            if (kind, n) in (("proj", 1), ("proj", 3), ("vproj", 1)):
                return attended[:, :]
            return shared[:, :]

        const_in = sem("const_in")
        table_in = sem("table_in")
        loads_over = sem("loads_over")
        const_ok = sem("const_ok")
        zero_ok = sem("zero_ok")
        x_in = [sem(f"x_in{i}") for i in range(2)]
        wb_in, wg_in, ffn_in = sem("wb_in"), sem("wg_in"), sem("ffn_in")
        ffn_hi = sem("ffn_hi")
        ffn_split = sem("ffn_split")
        bias_ok = sem("bias_ok")
        bias_added = sem("bias_added")
        var_ready = sem("var_ready")
        rstd_ready = sem("rstd_ready")
        stat_step = sem("stat_step")
        sqrt_done = sem("sqrt_done")
        xn_ready = sem("xn_ready")
        x_turned = sem("x_turned")
        x_hi = sem("x_hi")
        x_lo = sem("x_lo")
        base_done = sem("base_done")
        gate_done = sem("gate_done")
        gate_max = sem("gate_max")
        gate_exp = sem("gate_exp")
        gate_step = sem("gate_step")
        weight_step = sem("weight_step")
        gated_ready = sem("gated_ready")
        gated_turned = sem("gated_turned")
        gated_hi = sem("gated_hi")
        gated_lo = sem("gated_lo")
        moe_done = sem("moe_done")
        ffn_added = sem("ffn_added")
        wq_in, wk_in, wv_in, wo_in = sem("wq_in"), sem("wk_in"), sem("wv_in"), sem("wo_in")
        wq_split, wk_split, wv_split, wo_split = (sem("wq_split"), sem("wk_split"),
                                                  sem("wv_split"), sem("wo_split"))
        scored = sem("scored")
        max_ready = sem("max_ready")
        exp_done = sem("exp_done")
        block_turned = sem("block_turned")
        block_hi = sem("block_hi")
        block_lo = sem("block_lo")
        block_used = sem("block_used")
        rinv_ready = sem("rinv_ready")
        rinv_out = sem("rinv_out")
        rinv_in = sem("rinv_in")
        ctx_normed = sem("ctx_normed")
        ctx_hi = sem("ctx_hi")
        ctx_lo = sem("ctx_lo")
        proj_done = sem("proj_done")
        proj_biased = sem("proj_biased")
        bias_moved = sem("bias_moved")
        proj_cos = sem("proj_cos")
        proj_sin = sem("proj_sin")
        proj_rotated = sem("proj_rotated")
        proj_hi = sem("proj_hi")
        proj_lo = sem("proj_lo")
        v_done = sem("v_done")
        v_biased = sem("v_biased")
        v_turned = sem("v_turned")
        v_hi = sem("v_hi")
        v_lo = sem("v_lo")
        out_done = sem("out_done")
        out_added = sem("out_added")
        stored = [sem(f"stored{i}") for i in range(2)]

        def tile_no(G, r, i):
            return G * (RH * ST) + (r * ST + i)

        def slot_no(G, r, s):
            return G * (RH * SLOTS) + (r * SLOTS + s)

        def chunk_no(G, r, c):
            return G * (2 * RH) + (2 * r + c)

        def head_no(G, r):
            return G * RH + r

        def unit_no(G, j):
            return G * UNITS + j

        def v_no(G, k):
            return G * 2 + k

        def out_no(G, p, t):
            return G * (2 * ST) + (p * ST + t)

        def wait_shared_bank(eng, G, unit):
            kind = unit[0]
            if kind == "proj":
                eng.wait_ge(proj_biased, unit_no(G, unit[1]) + 1)
            elif kind == "vproj":
                eng.wait_ge(v_biased, v_no(G, unit[1]) + 1)
            elif kind == "vturn":
                eng.wait_ge(v_lo, v_no(G, unit[1]) + 1)
            else:
                eng.wait_ge(out_added, out_no(G, unit[1], unit[2]) + 1)

        block = ctx.enter_context(nc.Block())

        @block.sync
        def _(sp):
            sp.dma_start(ident[:, :], tables[:, 2 * S:2 * S + P]).then_inc(const_in, 16)
            sp.dma_start(mask[:, :], tables[:, 2 * S + P:2 * S + 2 * P]).then_inc(const_in, 16)
            sp.dma_start(bthr_wide[:, :], bthr.partition_broadcast(P)).then_inc(const_in, 16)

            def load_q(g, G, r, first=False):
                if not first:
                    sp.wait_ge(wq_split, head_no(G, r) * 2)
                sp.dma_start(wq_raw[:, :, :], wq[bass.ds(g * RH + r, 1), :, :, :]
                             .rearrange("o p k d -> (o p) k d")).then_inc(wq_in, 16)

            def load_k(g, G, ahead):
                if ahead:
                    sp.wait_ge(wk_split, (G + ahead) * 2)
                sp.dma_start(wk_raw[:, :, :], wk[bass.ds(g + ahead, 1), :, :, :]
                             .rearrange("o p k d -> (o p) k d")).then_inc(wk_in, 16)

            def load_v(g, G, ahead):
                if ahead:
                    sp.wait_ge(wv_split, (G + ahead) * 2)
                sp.dma_start(wv_raw[:, :, :], wv[bass.ds(g + ahead, 1), :, :, :]
                             .rearrange("o p k d -> (o p) k d")).then_inc(wv_in, 16)

            def load_o(g, G, p, first=False):
                if not first:
                    sp.wait_ge(wo_split, (G * 2 + p) * 2)
                sp.dma_start(wo_raw[:, :, :], wo[bass.ds(g * RH + 2 * p, 2), :, :]
                             .rearrange("h d n -> d h n")).then_inc(wo_in, 16)

            def load_x(b, t):
                sp.dma_start(acc[:, t, :], x[bass.ds(b, 1), t * P:(t + 1) * P, :]
                             .rearrange("o p n -> (o p) n")).then_inc(x_in[t // TC], 16)

            def spread_rinv(G, r, c):
                n = chunk_no(G, r, c)
                sp.wait_ge(rinv_ready, n + 1)
                sp.dma_start(rinv_row[c, :, :], rinv[:, c * TC:(c + 1) * TC]).then_inc(rinv_out, 16)
                sp.wait_ge(rinv_out, G * (2 * RH * 16) + (2 * r + c + 1) * 16)
                sp.dma_start(rinv_wide[:, c, :], rinv_row[c, :, :].rearrange("p t -> (p t)")
                             .partition_broadcast(P)).then_inc(rinv_in, 16)

            sp.sem_inc(stored[1], 1)
            with sp.Fori(0, B) as b:
                for t in range(TC):
                    load_x(b, t)
                sp.dma_start(wg_raw, wgate).then_inc(wg_in, 16)
                sp.dma_start(wb_raw, wbase).then_inc(wb_in, 16)
                sp.wait_ge(stored[1], b * (TC * 16) + 1)
                for t in range(TC, ST):
                    load_x(b, t)
                sp.dma_start(ba_raw, badapt).then_inc(ffn_in, 16)
                sp.dma_start(bias_sum, bbase.partition_broadcast(P)).then_inc(ffn_in, 16)
                sp.dma_start(bias_o, bo.partition_broadcast(P)).then_inc(ffn_in, 16)
                G0 = b * GROUPS
                load_k(0, G0, 0)
                load_v(0, G0, 0)
                load_q(0, G0, 0, True)
                load_q(0, G0, 1)

                def group(g, G, has_prev, has_next):
                    load_q(g, G, 2)
                    if has_next:
                        load_v(g, G, 1)
                    load_o(g, G, 0, not has_prev)
                    for r in range(RH):
                        spread_rinv(G, r, 0)
                        spread_rinv(G, r, 1)
                        if r == 1:
                            load_o(g, G, 1)
                            if has_next:
                                load_k(g, G, 1)
                        if r == 0 or r < RH - 1 and has_next:
                            load_q(g, G, r + 3)

                group(0, G0, False, True)
                with sp.Fori(1, GROUPS - 1) as g:
                    group(g, b * GROUPS + g, True, True)
                last = GROUPS - 1
                group(last, G0 + last, True, False)
                sp.wait_ge(stored[0], b * (TC * 16) + TC * 16)
                sp.sem_inc(loads_over, 1)
            sp.wait_ge(stored[1], B * TC * 16 + 1)

        @block.gpsimd
        def _(pool):
            def split(hi, lo, raw, done, count):
                zeros = zero[:, 0:1]
                for _ in raw.shape[2:]:
                    zeros = zeros.unsqueeze(2)
                pool.tensor_tensor(hi, raw, zeros.to_broadcast(list(raw.shape)), ALU.add)\
                    .then_inc(done, 1)
                pool.wait_ge(done, count + 1)
                pool.tensor_tensor(lo, raw, hi.bitcast(f32), ALU.subtract).then_inc(done, 1)

            def split_q(G, r):
                pool.wait_ge(wq_in, (head_no(G, r) + 1) * 16)
                ahead, r4 = divmod(r, RH)
                if r:
                    pool.wait_ge(proj_done, unit_no(G, UNITS * ahead + (2 + 2 * r4 if r4 else 0)))
                split(wq_parts[:, HI, :, :], wq_parts[:, LO, :, :], wq_raw[:, :, :],
                      wq_split, head_no(G, r) * 2)

            def split_k(G, ahead):
                pool.wait_ge(wk_in, (G + (ahead + 1)) * 16)
                if ahead:
                    pool.wait_ge(proj_done, unit_no(G, 3))
                split(wk_parts[:, HI, :, :], wk_parts[:, LO, :, :], wk_raw[:, :, :],
                      wk_split, (G + ahead) * 2)

            def split_v(G, ahead):
                pool.wait_ge(wv_in, (G + (ahead + 1)) * 16)
                if ahead:
                    pool.wait_ge(v_done, v_no(G, 2))
                split(wv_parts[:, HI, :, :], wv_parts[:, LO, :, :], wv_raw[:, :, :],
                      wv_split, (G + ahead) * 2)

            def split_o(G, p, has_prev):
                pool.wait_ge(wo_in, (G * 2 + (p + 1)) * 16)
                if has_prev:
                    pool.wait_ge(out_done, out_no(G, p - 1, 0))
                split(wo_parts[:, p, HI, :, :], wo_parts[:, p, LO, :, :], wo_raw[:, :, :],
                      wo_split, (G * 2 + p) * 2)

            def rotate(G, j):
                n, a = unit_no(G, j), j % 2
                c = proj_target(j)[1]
                pool.wait_ge(proj_biased, n + 1)
                if j >= 2:
                    pool.wait_ge(proj_lo, unit_no(G, j - 1))
                pool.tensor_tensor(rotated[:, a, :], biased[:, a, :],
                                   cos_sin[:, 0, c * CH:(c + 1) * CH], ALU.mult)\
                    .then_inc(proj_cos, 1)

            def rotated_low(G, j):
                what, c, _ = proj_target(j)
                to = (qT if what == "q" else kT)[:, :, c * CH:(c + 1) * CH]
                pool.wait_ge(proj_hi, unit_no(G, j) + 1)
                pool.tensor_tensor(to[:, LO, :], rotated[:, j % 2, :], to[:, HI, :].bitcast(f32),
                                   ALU.subtract).then_inc(proj_lo, 1)

            def ctx_low(G, r, c):
                to = ctxT[:, :, r % RH, c * CH:(c + 1) * CH]
                pool.wait_ge(ctx_hi, chunk_no(G, r, c) + 1)
                pool.tensor_tensor(to[:, LO, :], normed[:, :], to[:, HI, :].bitcast(f32),
                                   ALU.subtract).then_inc(ctx_lo, 1)

            def group(G, has_prev, has_next):
                for r in range(RH):
                    for s in range(SLOTS):
                        if s == 2 and (r or has_prev):
                            ctx_low(G, r - 1, 1)
                        if s == 6:
                            ctx_low(G, r, 0)
                        for u in units_of(r, s - PART_LAG, has_prev, has_next):
                            if u[0] == "proj":
                                rotated_low(G, u[1])
                        for u in units_of(r, s, has_prev, has_next):
                            if u[0] == "proj":
                                rotate(G, u[1])
                        if s == 9 and (r < 2 or has_next):
                            split_q(G, r + 2)
                        if s == 10 and r == 0 and has_next:
                            split_v(G, 1)
                        if s == 3 and r == 1:
                            split_o(G, 0, has_prev)
                        if s == 10 and r == 2 and has_next:
                            split_k(G, 1)
                        if s == 2 and r == 2:
                            split_o(G, 1, has_prev)

            pool.memset(zero[:, :], 0.0).then_inc(zero_ok, 1)
            pool.wait_ge(zero_ok, 1)
            with pool.Fori(0, B) as b:
                for n, (hi, lo, raw) in enumerate((
                        (wg_parts[:, HI, :, :], wg_parts[:, LO, :, :], wg_raw),
                        (wb_parts[:, HI, :, :], wb_parts[:, LO, :, :], wb_raw),
                        (ba_parts[:, HI, :], ba_parts[:, LO, :], ba_raw))):
                    pool.wait_ge(ffn_hi, b * 3 + (n + 1))
                    pool.tensor_tensor(lo, raw, hi.bitcast(f32), ALU.subtract)\
                        .then_inc(ffn_split, 1)
                pool.tensor_tensor(bias_sum, bias_sum, bias_o, ALU.add).then_inc(bias_ok, 1)
                pool.wait_ge(bias_ok, b + 1)
                G0 = b * GROUPS
                for t in range(ST):
                    pool.wait_ge(xn_ready, b * ST + (t + 1))
                    pool.tensor_tensor(acc[:, t, :], acc[:, t, :], bias_sum, ALU.add)\
                        .then_inc(bias_added, 1)
                    if t == TC:
                        split_k(G0, 0)
                        split_q(G0, 0)
                        split_v(G0, 0)
                pool.wait_ge(table_in, 16 * 2)
                rotate(G0, 0)
                for j in range(PRE_UNITS):
                    if j + 1 < PRE_UNITS:
                        rotate(G0, j + 1)
                    rotated_low(G0, j)
                split_q(G0, 1)
                group(G0, False, True)
                with pool.Fori(1, GROUPS - 1) as g:
                    group(b * GROUPS + g, True, True)
                group(G0 + (GROUPS - 1), True, False)
                ctx_low(G0 + (GROUPS - 1), RH - 1, 1)
                pool.wait_ge(out_done, b * (2 * GROUPS * ST) + 2 * GROUPS * ST)

        @block.scalar
        def _(act):
            def copy(to, source):
                return act.activation(to, source, ACT.Copy)

            def exponentials(G, r, i, first):
                n = (i + 1) * P
                c = i // TC
                act.wait_ge(max_ready, tile_no(G, r, i) + 1)
                if not first:
                    act.wait_ge(block_turned, slot_no(G, r - 1, i if c == 0 else TC + i) + 1)
                    if i % TC == 0:
                        act.wait_ge(rinv_ready, chunk_no(G, r - 1, c) + 1)
                act.activation(prob_tile(i)[:, 0:n], score_bank(i)[:, 0:n], ACT.Exp,
                               bias=neg_max[:, i:i + 1], accum_out=row_sum[:, i:i + 1])\
                   .then_inc(exp_done, 1)

            def block_high(G, r, s, first):
                a, at = s % 2, block_start(s)
                act.wait_ge(block_turned, slot_no(G, r, s) + 1)
                if not first or s >= LAG:
                    act.wait_ge(block_used, slot_no(G, r, s - LAG) + 1)
                copy(probT[:, a, HI, at:CH], turned[:, a, at:CH]).then_inc(block_hi, 1)

            def projected(G, j):
                what, _, r = proj_target(j)
                if j < PRE_UNITS:
                    column = bias[:, GROUPS * NB + (what == "k"):GROUPS * NB + 1 + (what == "k")]
                else:
                    column = bias_now[:, r - 1:r] if what == "q" else bias_now[:, RH:RH + 1]
                    act.wait_ge(bias_moved, G + 1)
                act.wait_ge(proj_done, unit_no(G, j) + 1)
                if j >= 2:
                    act.wait_ge(proj_cos, unit_no(G, j - 1))
                    act.wait_ge(proj_sin, unit_no(G, j - 1) * 2)
                act.activation(biased[:, j % 2, :], unit_bank("proj", j), ACT.Identity,
                               bias=column).then_inc(proj_biased, 1)

            def rotated_high(G, j):
                what, c, r = proj_target(j)
                to = (qT if what == "q" else kT)[:, HI, c * CH:(c + 1) * CH]
                act.wait_ge(proj_rotated, unit_no(G, j) + 1)
                if j >= PRE_UNITS:
                    i = TC - 1 if what == "q" and c == 0 else ST - 1
                    act.wait_ge(scored, tile_no(G, r - 1, i) + 1)
                copy(to, rotated[:, j % 2, :]).then_inc(proj_hi, 1)

            def v_projected(G, k):
                c = k % 2
                act.wait_ge(v_done, v_no(G, k) + 1)
                if k >= 2:
                    act.wait_ge(v_turned, v_no(G, k - 2) + 1)
                column = bias_now[:, RH + 1:RH + 2] if k >= 2 else bias[:, GROUPS * NB + 2:]
                act.activation(vT[:, c * CH:(c + 1) * CH], unit_bank("vproj", k), ACT.Identity,
                               bias=column).then_inc(v_biased, 1)

            def move_bias(g):
                copy(bias_now[:, :], bias[:, bass.ds(g * NB, NB)]).then_inc(bias_moved, 1)

            def v_high(G, k, has_prev):
                u = k % 2
                act.wait_ge(v_turned, v_no(G, k) + 1)
                if k > 1 or has_prev:
                    act.wait_ge(block_used, slot_no(G, (k // 2) * RH - 1, TC + TC * u + TC - 1) + 1)
                copy(v[:, HI, TC * u:TC * (u + 1), :].rearrange("p t d -> p (t d)"),
                     unit_bank("vturn", k)).then_inc(v_hi, 1)

            def ctx_high(G, r, c, has_prev):
                act.wait_ge(ctx_normed, chunk_no(G, r, c) + 1)
                if c == 0 and r % 2 == 0 and has_prev:
                    act.wait_ge(out_done, out_no(G, r // 2 - 1, 0))
                copy(ctxT[:, HI, r % RH, c * CH:(c + 1) * CH], normed[:, :]).then_inc(ctx_hi, 1)

            def group(G, g, has_prev, has_next):
                for r in range(RH):
                    first = not r and not has_prev
                    for s in range(SLOTS):
                        if s != 2:
                            block_high(G, r, s, first)
                        if s == 0:
                            if not first:
                                exponentials(G, r, TC, first)
                        elif score_tile(s - 1) is not None and s != 3:
                            ahead, i = score_tile(s - 1)
                            if not ahead or r < RH - 1 or has_next:
                                exponentials(G, r + ahead, i, first and not ahead)
                        if s == 2:
                            if not first:
                                ctx_high(G, r - 1, 1, has_prev)
                            block_high(G, r, s, first)
                            exponentials(G, r, TC + 3, first)
                        if s == 6:
                            ctx_high(G, r, 0, has_prev)
                        for u in units_of(r, s, has_prev, has_next):
                            if u[0] == "proj":
                                projected(G, u[1])
                            if u[0] == "vproj":
                                v_projected(G, u[1])
                            if u[0] == "vturn":
                                v_high(G, u[1], has_prev)
                        for u in units_of(r, s - PART_LAG, has_prev, has_next):
                            if u[0] == "proj":
                                rotated_high(G, u[1])
                        if r == RH - 1 and s == SLOTS - 2 and has_next:
                            move_bias(g + 1)

            def square_root(b, h):
                act.wait_ge(var_ready, b * 2 + (h + 1))
                act.activation(rstd[:, 1, TC * h:TC * h + TC], rstd[:, 0, TC * h:TC * h + TC],
                               ACT.Sqrt).then_inc(sqrt_done, 1)

            act.wait_ge(x_in[1], TC * 16)
            act.dma_start(cos_sin[:, :, :], tables[:, 0:2 * S].rearrange("p (a s) -> p a s", a=2))\
               .then_inc(table_in, 16)
            act.dma_start(bias[:, :], bqkv).then_inc(table_in, 16)
            with act.Fori(0, B) as b:
                act.wait_ge(wg_in, b * 16 + 16)
                copy(wg_parts[:, HI, :, :], wg_raw).then_inc(ffn_hi, 1)
                square_root(b, 0)
                act.wait_ge(wb_in, b * 16 + 16)
                copy(wb_parts[:, HI, :, :], wb_raw).then_inc(ffn_hi, 1)
                for k in range(ST + 2):
                    T = b * ST + k
                    if k < ST:
                        act.wait_ge(x_turned, T + 1)
                        copy(xnT[:, HI, :, k * P:(k + 1) * P],
                             turned[:, k % 2, :].rearrange("p (k s) -> p k s", k=KT))\
                            .then_inc(x_hi, 1)
                    if k == 1:
                        square_root(b, 1)
                        act.wait_ge(ffn_in, b * (16 * 3) + 16 * 3)
                        copy(ba_parts[:, HI, :], ba_raw).then_inc(ffn_hi, 1)
                    if k >= 2:
                        act.wait_ge(gated_turned, T - 1)
                        if k > 2:
                            act.wait_ge(moe_done, T - 2)
                        copy(gated_parts[:, HI, :], shared[:, 0:P]).then_inc(gated_hi, 1)
                    if 1 <= k <= ST:
                        bank = scores[:, 2 + (k - 1) % 2, :]
                        act.wait_ge(gate_max, T)
                        act.activation(gate[:, 0, :], bank[:, E * R:E * R + E], ACT.Exp,
                                       bias=thr[:, 0:1], accum_out=thr[:, 1:2])\
                           .then_inc(gate_exp, 1)
                        act.activation(thr[:, 2:3], bank[:, E * R + E:E * R + E + 1], ACT.Exp,
                                       bias=neg_bthr[:, 0:1], scale=-1.0).then_inc(gate_exp, 1)
                G0 = b * GROUPS
                act.wait_ge(table_in, 16 * 2)
                projected(G0, 0)
                projected(G0, 1)
                rotated_high(G0, 0)
                projected(G0, 2)
                rotated_high(G0, 1)
                projected(G0, 3)
                rotated_high(G0, 2)
                v_projected(G0, 0)
                v_projected(G0, 1)
                rotated_high(G0, 3)
                v_high(G0, 0, False)
                move_bias(0)
                for i in range(TC + 1):
                    exponentials(G0, 0, i, True)
                group(G0, 0, False, True)
                with act.Fori(1, GROUPS - 1) as g:
                    group(b * GROUPS + g, g, True, True)
                group(G0 + (GROUPS - 1), GROUPS - 1, True, False)
                ctx_high(G0 + (GROUPS - 1), RH - 1, 1, True)
                for t in range(ST):
                    act.wait_ge(out_added, out_no(G0 + (GROUPS - 1), 1, t) + 1)
                    act.dma_start(out[bass.ds(b, 1), t * P:(t + 1) * P, :]
                                  .rearrange("o p n -> (o p) n"), acc[:, t, :])\
                       .then_inc(stored[t // TC], 16)

        @block.vector
        def _(dve):
            def row_max(G, r, i):
                dve.wait_ge(scored, tile_no(G, r, i) + 1)
                dve.reduce_max(neg_max[:, i:i + 1], score_bank(i)[:, 0:(i + 1) * P], AX.X,
                               negate=True).then_inc(max_ready, 1)

            def inverse(G, r, c, first):
                dve.wait_ge(exp_done, tile_no(G, r, TC * c + TC - 1) + 1)
                if not first:
                    dve.wait_ge(ctx_normed, chunk_no(G, r - 1, c) + 1)
                dve.reciprocal(rinv[:, TC * c:TC * c + TC], row_sum[:, TC * c:TC * c + TC])\
                   .then_inc(rinv_ready, 1)

            def block_low(G, r, s):
                a, at = s % 2, block_start(s)
                dve.wait_ge(block_hi, slot_no(G, r, s) + 1)
                dve.tensor_tensor(probT[:, a, LO, at:CH], turned[:, a, at:CH],
                                  probT[:, a, HI, at:CH].bitcast(f32), ALU.subtract)\
                   .then_inc(block_lo, 1)

            def cross(G, j):
                n, a = unit_no(G, j), j % 2
                c = proj_target(j)[1]
                half = D // 2
                dve.wait_ge(proj_biased, n + 1)
                if j >= 2:
                    dve.wait_ge(proj_rotated, unit_no(G, j - 1))
                for to, of in ((0, half), (half, 0)):
                    dve.tensor_tensor(crossed[to:to + half, a, :], biased[of:of + half, a, :],
                                      cos_sin[of:of + half, 1, c * CH:(c + 1) * CH], ALU.mult)\
                       .then_inc(proj_sin, 1)

            def rotate(G, j):
                n, a = unit_no(G, j), j % 2
                dve.wait_ge(proj_cos, n + 1)
                dve.wait_ge(proj_sin, n * 2 + 2)
                dve.tensor_tensor(rotated[:, a, :], rotated[:, a, :], crossed[:, a, :], ALU.add)\
                   .then_inc(proj_rotated, 1)

            def v_low(G, k):
                u = k % 2
                dve.wait_ge(v_hi, v_no(G, k) + 1)
                to = v[:, :, TC * u:TC * (u + 1), :].rearrange("p a t d -> p a (t d)")
                dve.tensor_tensor(to[:, LO, :], unit_bank("vturn", k), to[:, HI, :].bitcast(f32),
                                  ALU.subtract).then_inc(v_lo, 1)

            def normalise(G, r, c, first=False):
                n = chunk_no(G, r, c)
                dve.wait_ge(block_used, slot_no(G, r, TC - 1 if c == 0 else SLOTS - 1) + 1)
                dve.wait_ge(rinv_in, (n + 1) * 16)
                if not first:
                    dve.wait_ge(ctx_lo, n)
                dve.tensor_tensor(normed[:, :].rearrange("p (t q) -> p t q", t=TC),
                                  attended[:, :].rearrange("p (t q) -> p t q", t=TC),
                                  rinv_wide[:, c, :].rearrange("p (q t) -> p t q", t=TC),
                                  ALU.mult)\
                   .then_inc(ctx_normed, 1)

            def add_out(G, p, t, bank=shared[:, :]):
                dve.wait_ge(out_done, out_no(G, p, t) + 1)
                dve.wait_ge(out_added, out_no(G, p - 1, t) + 1)
                dve.tensor_tensor(acc[:, t, :], acc[:, t, :], bank, ALU.add)\
                   .then_inc(out_added, 1)

            def add_out_first(G, t):
                dve.wait_ge(out_done, out_no(G, 0, t) + 1)
                dve.tensor_tensor(acc[:, t, :], acc[:, t, :], shared[:, :], ALU.add)\
                   .then_inc(out_added, 1)

            def group(G, has_prev, has_next):
                for r in range(RH):
                    first = not r and not has_prev
                    for s in range(SLOTS):
                        if s in (0, 4):
                            inverse(G, r, s // TC, first)
                        if s == 1 and not first:
                            normalise(G, r - 1, 1)
                        if s == 5:
                            normalise(G, r, 0, first)
                        if s == 2:
                            row_max(G, r, TC + 3)
                        block_low(G, r, s)
                        for u in units_of(r, s - 2, has_prev, has_next):
                            if u[0] == "proj":
                                rotate(G, u[1])
                        if score_tile(s) is not None and s != 2:
                            ahead, i = score_tile(s)
                            if not ahead or r < RH - 1 or has_next:
                                row_max(G, r + ahead, i)
                        for u in units_of(r, s - 1, has_prev, has_next):
                            if u[0] == "proj":
                                cross(G, u[1])
                        for u in units_of(r, s, has_prev, has_next):
                            if u[0] == "vturn":
                                v_low(G, u[1])
                            if u[0] == "out":
                                if has_prev:
                                    add_out(G, u[1], u[2])
                                else:
                                    add_out_first(G, u[2])

            dve.wait_ge(const_in, 16 * 3)
            dve.tensor_copy(ident_b[:, :], ident[:, :]).then_inc(const_ok, 1)
            dve.tensor_copy(mask_b[:, :], mask[:, :]).then_inc(const_ok, 1)
            dve.tensor_scalar(neg_bthr[:, 0:1], bthr_wide[:, :], -1.0, None, ALU.mult)\
               .then_inc(const_ok, 1)
            with dve.Fori(0, B) as b:
                def chained(instruction, done, count):
                    instruction.then_inc(done, 1)
                    dve.wait_ge(done, count)

                def statistics(h):
                    four = slice(TC * h, TC * h + TC)
                    dve.wait_ge(x_in[h], b * (TC * 16) + TC * 16)
                    for t in range(4 * h, 4 * h + 4):
                        last = dve.bn_stats(stats[:, t, :], acc[:, t, :])
                    chained(last, stat_step, b * 14 + (7 * h + 1))
                    even, odd = stats[:, four, 0:3], stats[:, four, 3:6]
                    dve.tensor_tensor(moments[:, 0, four], even[:, :, 1], odd[:, :, 1], ALU.add)
                    dve.tensor_tensor(moments[:, 1, four], even[:, :, 1], odd[:, :, 1],
                                      ALU.subtract)
                    chained(dve.tensor_tensor(moments[:, 2, four], even[:, :, 2], odd[:, :, 2],
                                              ALU.add), stat_step, b * 14 + (7 * h + 2))
                    dve.tensor_scalar(moments[:, 3, four], moments[:, 0, four], 0.5, None,
                                      ALU.mult)
                    dve.tensor_tensor(moments[:, 4, four], moments[:, 1, four],
                                      moments[:, 1, four], ALU.mult)
                    chained(dve.tensor_scalar(moments[:, 5, four], moments[:, 2, four],
                                              1.0 / HID, EPS, ALU.mult, ALU.add),
                            stat_step, b * 14 + (7 * h + 3))
                    chained(dve.scalar_tensor_tensor(rstd[:, 0, four], moments[:, 4, four], 0.25,
                                                     moments[:, 5, four], ALU.mult, ALU.add),
                            var_ready, b * 2 + (h + 1))
                    dve.wait_ge(sqrt_done, b * 2 + (h + 1))
                    chained(dve.reciprocal(rstd[:, 2, four], rstd[:, 1, four]),
                            stat_step, b * 14 + (7 * h + 4))
                    chained(dve.tensor_tensor(rstd[:, 3, four], rstd[:, 2, four],
                                              rstd[:, 2, four], ALU.mult),
                            stat_step, b * 14 + (7 * h + 5))
                    chained(dve.tensor_tensor(rstd[:, 3, four], rstd[:, 3, four],
                                              rstd[:, 0, four], ALU.mult),
                            stat_step, b * 14 + (7 * h + 6))
                    chained(dve.tensor_scalar(rstd[:, 3, four], rstd[:, 3, four], -0.5, 1.5,
                                              ALU.mult, ALU.add),
                            stat_step, b * 14 + (7 * h + 7))
                    chained(dve.tensor_tensor(rstd[:, 2, four], rstd[:, 2, four],
                                              rstd[:, 3, four], ALU.mult),
                            rstd_ready, b * 2 + (h + 1))

                def normalised(t):
                    T = b * ST + t
                    if t >= 2:
                        dve.wait_ge(x_turned, T - 1)
                    dve.tensor_scalar(xn[:, t % 2, :], acc[:, t, :], moments[:, 3, t:t + 1],
                                      rstd[:, 2, t:t + 1], ALU.subtract, ALU.mult)\
                       .then_inc(xn_ready, 1)

                def gating(t):
                    T = b * ST + t
                    bank = scores[:, 2 + t % 2, :]

                    def step(instruction, k):
                        chained(instruction, gate_step, T * 7 + k)
                    dve.wait_ge(gate_done, T + 1)
                    dve.reduce_max(thr[:, 0:1], bank[:, E * R:E * R + E], AX.X, negate=True)\
                       .then_inc(gate_max, 1)
                    dve.wait_ge(gate_exp, T * 2 + 2)
                    dve.reciprocal(thr[:, 3:4], thr[:, 1:2])
                    step(dve.tensor_scalar(thr[:, 4:5], thr[:, 2:3], 1.0, None, ALU.add), 1)
                    step(dve.reciprocal(thr[:, 5:6], thr[:, 4:5]), 2)
                    step(dve.tensor_scalar(thr[:, 6:7], thr[:, 5:6], MAX_THR, None, ALU.mult), 3)
                    step(dve.tensor_scalar(gate[:, 1, :], gate[:, 0, :], thr[:, 3:4], thr[:, 6:7],
                                           ALU.mult, ALU.subtract), 4)
                    step(dve.tensor_scalar(gate[:, 2, :], gate[:, 1, :], 0.0, None, ALU.max), 5)
                    step(dve.reduce_sum(thr[:, 7:8], gate[:, 2, :], AX.X), 6)
                    step(dve.scalar_tensor_tensor(thr[:, 8:9], thr[:, 7:8], 0.0, thr[:, 7:8],
                                                  ALU.is_equal, ALU.add), 7)
                    chained(dve.reciprocal(thr[:, 9:10], thr[:, 8:9]), weight_step, T * 2 + 1)
                    chained(dve.tensor_scalar(gate[:, 3, :], gate[:, 2, :], thr[:, 9:10], SCALING,
                                              ALU.mult, ALU.mult), weight_step, T * 2 + 2)
                    if t >= 2:
                        dve.wait_ge(gated_turned, T - 1)
                    dve.tensor_tensor(gated[:, t % 2, :].rearrange("p (e r) -> p e r", e=E),
                                      bank[:, 0:E * R].rearrange("p (e r) -> p e r", e=E),
                                      gate[:, 3, :].unsqueeze(2).to_broadcast([P, E, R]),
                                      ALU.mult).then_inc(gated_ready, 1)

                statistics(0)
                normalised(0)
                for k in range(ST + 2):
                    T = b * ST + k
                    if k + 1 < ST:
                        normalised(k + 1)
                    if k < ST:
                        dve.wait_ge(x_hi, T + 1)
                        part = xnT[:, :, :, k * P:(k + 1) * P]
                        dve.tensor_tensor(part[:, LO, :, :],
                                          turned[:, k % 2, :].rearrange("p (k s) -> p k s", k=KT),
                                          part[:, HI, :, :].bitcast(f32), ALU.subtract)\
                           .then_inc(x_lo, 1)
                    if k == 1:
                        statistics(1)
                    if k >= 2:
                        dve.wait_ge(gated_hi, T - 1)
                        dve.tensor_tensor(gated_parts[:, LO, :], shared[:, 0:P],
                                          gated_parts[:, HI, :].bitcast(f32), ALU.subtract)\
                           .then_inc(gated_lo, 1)
                    if 1 <= k <= ST:
                        gating(k - 1)
                    if k >= 2:
                        t = k - 2
                        dve.wait_ge(moe_done, T - 1)
                        dve.wait_ge(bias_added, T - 1)
                        dve.tensor_tensor(acc[:, t, :], acc[:, t, :], scores[:, t % 2, :], ALU.add)\
                           .then_inc(ffn_added, 1)
                G0 = b * GROUPS
                dve.wait_ge(table_in, 16 * 2)
                cross(G0, 0)
                for j in range(PRE_UNITS):
                    if j + 1 < PRE_UNITS:
                        cross(G0, j + 1)
                    rotate(G0, j)
                v_low(G0, 0)
                for i in range(TC + 1):
                    row_max(G0, 0, i)
                dve.wait_ge(ffn_added, b * ST + ST)
                group(G0, False, True)
                with dve.Fori(1, GROUPS - 1) as g:
                    group(b * GROUPS + g, True, True)
                last = G0 + (GROUPS - 1)
                group(last, True, False)
                normalise(last, RH - 1, 1)
                for t in range(TC, ST):
                    add_out(last, 1, t, scores[:, t % TC, :])

        @block.tensor
        def _(pe):
            def product(to, lhs, rhs, first=True, last=True):
                for n, (a, c) in enumerate(((HI, HI), (HI, LO), (LO, HI))):
                    mm = pe.matmul(to, lhs[a], rhs[c], start=first and n == 0,
                                   stop=last and n == 2)
                return mm

            def parts(t, *at):
                return t[(slice(None), HI, *at)], t[(slice(None), LO, *at)]

            def score(G, r, i, first):
                c = i // TC
                if i % TC == 0:
                    ahead, r4 = divmod(r, RH)
                    j = UNITS * ahead + (1 + 2 * c if r4 == 0 else 2 + 2 * r4 + c)
                    pe.wait_ge(proj_lo, unit_no(G, j) + 1)
                if c == 0 and not first:
                    pe.wait_ge(exp_done, tile_no(G, r - 1, 6 + i // 2) + 1)
                if c == 1:
                    pe.wait_ge(exp_done, tile_no(G, r, (1, 3, 4, 5)[i - TC]) + 1)
                bank = score_bank(i)
                q = parts(qT, slice(i * P, (i + 1) * P))
                n = (i + 1) * P
                for at in range(0, n, CH):
                    to = min(at + CH, n)
                    diagonal = to == n
                    mm = product(bank[:, at:to], q, parts(kT, slice(at, to)), last=not diagonal)
                    if diagonal:
                        mm = pe.matmul(bank[:, n - P:n], ident_b[:, :], mask_b[:, :],
                                       start=False, stop=True)
                mm.then_inc(scored, 1)

            def turn_block(G, r, s, first):
                c, j = chunk_block(s)
                if s in (0, TC):
                    pe.wait_ge(exp_done, tile_no(G, r, TC * c + TC - 1) + 1)
                if not first or s >= LAG:
                    pe.wait_ge(block_lo, slot_no(G, r, s - LAG) + 1)
                for i in range(block_start(s) // P, TC):
                    mm = pe.matmul(turned[:, s % 2, i * P:(i + 1) * P],
                                   prob_tile(TC * c + i)[:, j * P:(j + 1) * P], ident[:, :],
                                   is_transpose=True)
                mm.then_inc(block_turned, 1)

            def attend(G, r, s, first):
                c, j = chunk_block(s)
                if j == 0 and not (first and c == 0):
                    pe.wait_ge(ctx_normed, chunk_no(G, r, c))
                if r == 0 and s in (0, TC + TC):
                    pe.wait_ge(v_lo, v_no(G, s // (2 * TC)) + 1)
                pe.wait_ge(block_lo, slot_no(G, r, s) + 1)
                at = block_start(s)
                product(attended[:, at:CH], parts(v, j),
                        (probT[:, s % 2, HI, at:CH], probT[:, s % 2, LO, at:CH]),
                        first=j == 0, last=j == TC * c + TC - 1).then_inc(block_used, 1)

            def project(G, j):
                what, c, r = proj_target(j)
                bank = unit_bank("proj", j)
                if what == "q":
                    pe.wait_ge(wq_split, head_no(G, r) * 2 + 2)
                    w = wq_parts
                else:
                    pe.wait_ge(wk_split, (G + r // RH) * 2 + 2)
                    w = wk_parts
                for k in range(KT):
                    mm = product(bank, parts(w, k),
                                 parts(xnT, k, slice(c * CH, (c + 1) * CH)),
                                 first=k == 0, last=k == KT - 1)
                mm.then_inc(proj_done, 1)

            def project_v(G, k):
                c = k % 2
                bank = unit_bank("vproj", k)
                pe.wait_ge(wv_split, (G + k // 2) * 2 + 2)
                for b in range(KT):
                    mm = product(bank, parts(wv_parts, b),
                                 parts(xnT, b, slice(c * CH, (c + 1) * CH)),
                                 first=b == 0, last=b == KT - 1)
                mm.then_inc(v_done, 1)

            def turn_v(G, k):
                u = k % 2
                bank = unit_bank("vturn", k)
                pe.wait_ge(v_biased, v_no(G, k) + 1)
                for i in range(TC):
                    mm = pe.matmul(bank[:, i * P:(i + 1) * P],
                                   vT[:, (TC * u + i) * P:(TC * u + i + 1) * P], ident[:, :],
                                   is_transpose=True)
                mm.then_inc(v_turned, 1)

            def project_out(G, p, t, bank=shared[:, :]):
                pe.wait_ge(ctx_lo, chunk_no(G, 2 * p + 1, t // TC) + 1)
                pe.wait_ge(wo_split, G * 4 + (2 * p + 2))
                for h in range(2):
                    r = (2 * p + h) % RH
                    mm = product(bank, parts(ctxT, r, slice(t * P, (t + 1) * P)),
                                 (wo_parts[:, p % 2, HI, h, :], wo_parts[:, p % 2, LO, h, :]),
                                 first=h == 0, last=h == 1)
                mm.then_inc(out_done, 1)

            def unit(G, u):
                if u[0] == "proj":
                    project(G, u[1])
                elif u[0] == "vproj":
                    project_v(G, u[1])
                elif u[0] == "vturn":
                    turn_v(G, u[1])
                else:
                    project_out(G, u[1], u[2])

            def group(G, has_prev, has_next):
                previous = ("vturn", 0)
                for r in range(RH):
                    first = not r and not has_prev
                    for s in range(SLOTS):
                        turn_block(G, r, s, first)
                        if s == 2:
                            score(G, r, TC + 3, False)
                        if s >= LAG:
                            attend(G, r, s - LAG, first)
                        elif not first:
                            attend(G, r - 1, s - LAG + SLOTS, False)
                        if score_tile(s) is not None and s != 2:
                            ahead, i = score_tile(s)
                            if not ahead or r < RH - 1 or has_next:
                                score(G, r + ahead, i, False)
                        for u in units_of(r, s, has_prev, has_next):
                            wait_shared_bank(pe, G, previous)
                            unit(G, u)
                            previous = u

            pe.wait_ge(const_ok, 3)
            with pe.Fori(0, B) as b:
                for k in range(ST + 2):
                    T = b * ST + k
                    if k < ST:
                        pe.wait_ge(xn_ready, T + 1)
                        if k >= 2:
                            pe.wait_ge(x_lo, T - 1)
                        for i in range(KT):
                            mm = pe.matmul(turned[:, k % 2, i * P:(i + 1) * P],
                                           xn[:, k % 2, i * P:(i + 1) * P], ident[:, :],
                                           is_transpose=True)
                        mm.then_inc(x_turned, 1)
                    if k >= 2:
                        pe.wait_ge(gated_ready, T - 1)
                        if k > 2:
                            pe.wait_ge(gated_lo, T - 2)
                        pe.matmul(shared[:, 0:P], gated[:, k % 2, :], ident[:, :],
                                  is_transpose=True).then_inc(gated_turned, 1)
                    if 1 <= k <= ST:
                        t = k - 1
                        if t == 0:
                            pe.wait_ge(ffn_split, b * 3 + 1)
                        pe.wait_ge(x_lo, T)
                        tile = slice(t * P, (t + 1) * P)
                        if t >= 2:
                            pe.wait_ge(gated_ready, T - 2)
                        for i in range(KT):
                            mm = product(scores[:, 2 + t % 2, 0:NGATE], parts(xnT, i, tile),
                                         (wg_parts[:, HI, i, :], wg_parts[:, LO, i, :]),
                                         first=i == 0, last=i == KT - 1)
                        mm.then_inc(gate_done, 1)
                        if t == 0:
                            pe.wait_ge(ffn_split, b * 3 + 2)
                        if t >= 2:
                            pe.wait_ge(ffn_added, T - 2)
                        for i in range(KT):
                            product(scores[:, t % 2, :], parts(xnT, i, tile),
                                    (wb_parts[:, HI, i, :], wb_parts[:, LO, i, :]),
                                    first=i == 0, last=False)
                    if k == 2:
                        pe.wait_ge(ffn_split, b * 3 + 3)
                    if k >= 2:
                        pe.wait_ge(gated_lo, T - 1)
                        product(scores[:, k % 2, :],
                                (gated_parts[:, HI, :], gated_parts[:, LO, :]),
                                (ba_parts[:, HI, :], ba_parts[:, LO, :]),
                                first=False).then_inc(moe_done, 1)
                G0 = b * GROUPS
                for j in range(PRE_UNITS):
                    if j >= 2:
                        wait_shared_bank(pe, G0, ("proj", j - 2))
                    project(G0, j)
                wait_shared_bank(pe, G0, ("proj", PRE_UNITS - 2))
                project_v(G0, 0)
                wait_shared_bank(pe, G0, ("proj", PRE_UNITS - 1))
                project_v(G0, 1)
                turn_v(G0, 0)
                pe.wait_ge(ffn_added, b * ST + ST)
                for i in range(TC + 1):
                    score(G0, 0, i, True)
                group(G0, False, True)
                with pe.Fori(1, GROUPS - 1) as g:
                    group(b * GROUPS + g, True, True)
                last = G0 + (GROUPS - 1)
                group(last, True, False)
                for s in (SLOTS - 2, SLOTS - 1):
                    attend(last, RH - 1, s, False)
                for t in range(TC, ST):
                    project_out(last, 1, t, scores[:, t % TC, :])


def position_tables():
    import numpy as np

    half = D // 2
    inv_freq = (1.0 / np.power(np.float32(10000.0),
                               np.arange(half, dtype=np.float32) / np.float32(half))).astype(np.float32)
    angle = (np.arange(S, dtype=np.float32)[None, :] * inv_freq[:, None]).astype(np.float32)
    scale = float(D) ** -0.25
    cos = np.cos(angle.astype(np.float64)) * scale
    sin = np.sin(angle.astype(np.float64)) * scale
    tables = np.zeros((P, 2 * S + 2 * P), np.float32)
    tables[:half, 0:S] = tables[half:, 0:S] = cos
    tables[:half, S:2 * S] = sin
    tables[half:, S:2 * S] = -sin
    tables[:, 2 * S:2 * S + P] = np.eye(P)
    tables[:, 2 * S + P:] = np.where(np.tril(np.ones((P, P), bool)), 0.0, -1e30)
    return tables


def kernel(**inputs):
    import numpy as np
    import concourse.bacc as bacc
    from concourse.bass_utils import run_bass_kernel_spmd

    a = {n: np.asarray(v) for n, v in inputs.items()}

    def by_rows(w, n):
        return w.reshape(KT, P, n, D).transpose(2, 1, 0, 3)

    gate_cols = np.concatenate([a["L0_ffn_A"].reshape(E * R, HID), a["L0_ffn_W_gate"],
                                a["L0_ffn_W_thr"], np.zeros((1, HID), np.float32)]).T
    bq, bk, bv = (a[f"L0_attn_b{n}"].reshape(-1, D) for n in "qkv")
    bias_rows = []
    for g in range(GROUPS):
        n = (g + 1) % GROUPS
        bias_rows += [bq[g * RH + 1], bq[g * RH + 2], bq[g * RH + 3], bq[n * RH], bk[n], bv[n]]
    bias_rows += [bq[0], bk[0], bv[0]]
    arrays = {
        "in_x": a["L0_attn_hidden_states"],
        "in_wq": by_rows(a["L0_attn_Wq"], H),
        "in_wk": by_rows(a["L0_attn_Wk"], GROUPS),
        "in_wv": by_rows(a["L0_attn_Wv"], GROUPS),
        "in_wo": a["L0_attn_Wo"].reshape(H, D, HID),
        "in_bqkv": np.stack(bias_rows).T,
        "in_bo": a["L0_attn_bo"],
        "in_wbase": a["L0_ffn_W_base"].T.reshape(KT, P, HID).transpose(1, 0, 2),
        "in_bbase": a["L0_ffn_b_base"],
        "in_wgate": gate_cols.reshape(KT, P, NGATE).transpose(1, 0, 2),
        "in_bthr": a["L0_ffn_b_thr"],
        "in_badapt": a["L0_ffn_B"].transpose(0, 2, 1).reshape(E * R, HID),
        "in_tables": position_tables(),
    }
    arrays = {n: np.ascontiguousarray(v) for n, v in arrays.items()}
    nc = bacc.Bacc("TRN2", target_bir_lowering=False, num_devices=1)
    f32 = mybir.dt.float32
    args = [nc.dram_tensor(n, v.shape, f32, kind="ExternalInput").ap() for n, v in arrays.items()]
    args.append(nc.dram_tensor("rinv_row", (2, P, TC), f32, kind="Internal").ap())
    args.append(nc.dram_tensor("out", (B, S, HID), f32, kind="ExternalOutput").ap())
    build(nc, *args)
    return run_bass_kernel_spmd(nc, [arrays], core_ids=[0]).results[0]["out"]
```

```python
import concourse.bass as bass
from concourse import mybir
from contextlib import ExitStack

B, S, HID = 2, 1024, 512
H, GROUPS, D = 32, 8, 128
RH = H // GROUPS
E, R = 8, 16
P = 128
KT = HID // P
ST = S // P
CH = 512
TC = CH // P
SLOTS = TC + ST
LAG = 2
PROJ_SLOTS = ((2, 5), (1, 3), (2, 4), (0, 1, 3, 5))
OUT_SLOTS = ((1, 3, 8, 9, 10, 11), (9, 11), (1, 5, 7, 9, 10, 11), (7, 9))
LAST_OUT_SLOTS = (2, 4, 8, 9, 10, 11)
STAT_GROUPS = ((0, 1), (1, TC), (TC, ST))
NGATE = E * R + E + 2
NB = RH + 2
EPS = 1e-5
MAX_THR = 1.0 / 8.0
SCALING = 2.0
UNITS = 2 * RH + 2
PRE_UNITS = 4


def stat_group(t):
    return [start <= t < end for start, end in STAT_GROUPS].index(True)


def chunk_block(s):
    return (0, s) if s < TC else (1, s - TC)


def block_start(s):
    c, j = chunk_block(s)
    return max(j - TC * c, 0) * P


def score_tile(s):
    if s < 3:
        return False, TC + 1 + s
    if 7 <= s < 11:
        return True, s - 7
    if s == 11:
        return True, TC
    return None


def units_of(r, s, has_prev, has_next):
    found = []
    if r == 0 and s == 6:
        found.append(("vturn", 1))
    if (r < RH - 1 or has_next) and s in PROJ_SLOTS[r]:
        found.append(("proj", PRE_UNITS + 2 * r + PROJ_SLOTS[r].index(s)))
    if r == 1 and has_next and s in (5, 7):
        found.append(("vproj", 2 + s // 7))
    if r == RH - 1 and has_next and s == 11:
        found.append(("vturn", 2))
    if r >= 2 or has_prev:
        slots = OUT_SLOTS[r]
        if r == RH - 1 and not has_next:
            if s in LAST_OUT_SLOTS:
                n = LAST_OUT_SLOTS.index(s)
                found.append(("out", 0, ST - 2 + n) if n < 2 else ("out", 1, n - 2))
        elif s in slots:
            found.append(("out", 0 if r >= 2 else -1,
                          (len(OUT_SLOTS[r - 1]) if r % 2 else 0) + slots.index(s)))
    return found


def units_cut(r, s, has_prev, has_next):
    units = units_of(r, s - 2, has_prev, has_next) if s - 2 < 5 else []
    if s - 3 >= 5:
        units += units_of(r, s - 3, has_prev, has_next)
    return [u for u in units if u[0] == "proj"]


def proj_target(j):
    ahead, j = divmod(j, UNITS)
    if j < PRE_UNITS:
        return ("k", "q")[j % 2], j // 2, ahead * RH
    return "q", j % 2, (j - PRE_UNITS) // 2 + 1 + ahead * RH


def build(nc, x, wq, wk, wv, wo, bqkv, bo, wbase, bbase, wgate, bthr, badapt, tables, rinv_row, out):
    f32, f32r, bf16 = mybir.dt.float32, mybir.dt.float32r, mybir.dt.bfloat16
    ALU = mybir.AluOpType
    ACT = mybir.ActivationFunctionType
    AX = mybir.AxisListType
    ctx = ExitStack()
    with ctx:
        def sb(name, shape, dt=f32):
            return ctx.enter_context(nc.sbuf_tensor(name, shape, dt))

        def sem(name):
            return ctx.enter_context(nc.semaphore(name))

        HI, LO = 0, 1
        xnT = sb("xnT", [P, 2, KT, S], f32r)
        kT = sb("kT", [P, 2, S], f32r)
        qT = sb("qT", [P, 2, S], f32r)
        v = sb("v", [P, 2, ST, D], f32r)
        ctxT = sb("ctxT", [P, 2, RH, S], f32r)
        acc = sb("acc", [P, ST, HID])
        prob = sb("prob", [P, TC * CH + TC * S])
        probT = sb("probT", [P, LAG, 2, CH], f32r)
        wo_parts = sb("wo_parts", [P, 2, 2, 2, HID], f32r)
        wq_parts = sb("wq_parts", [P, 2, KT, D], f32r)
        wk_parts = sb("wk_parts", [P, 2, KT, D], f32r)
        wv_parts = sb("wv_parts", [P, 2, KT, D], f32r)
        wq_raw = sb("wq_raw", [P, KT, D])
        wk_raw = sb("wk_raw", [P, KT, D])
        wv_raw = sb("wv_raw", [P, KT, D])
        wo_raw = sb("wo_raw", [P, 2, HID])
        biased = sb("biased", [P, 2, CH])
        rotated = sb("rotated", [P, 2, CH])
        crossed = sb("crossed", [P, 2, CH])
        vT = sb("vT", [P, S])
        rinv_wide = sb("rinv_wide", [P, 2, CH])
        normed = sb("normed", [P, CH])
        cos_sin = sb("cos_sin", [P, 2, S])
        ident = sb("ident", [P, P])
        ident_b = sb("ident_b", [P, P], bf16)
        mask = sb("mask", [P, P])
        mask_b = sb("mask_b", [P, P], bf16)
        bias = sb("bias", [P, GROUPS * NB + 3])
        bias_now = sb("bias_now", [P, NB])
        neg_max = sb("neg_max", [P, ST])
        row_sum = sb("row_sum", [P, ST])
        rinv = sb("rinv", [P, ST])
        stats = sb("stats", [P, ST, 6])
        moments = sb("moments", [P, 6, ST])
        rstd = sb("rstd", [P, 6, ST])
        gate = sb("gate", [P, 6, E])
        thr = sb("thr", [P, 10])
        zero = sb("zero", [P, 1])
        minus_half = sb("minus_half", [P, ST])
        neg_bthr = sb("neg_bthr", [P, 1])
        bthr_wide = sb("bthr_wide", [P, 1])

        def prob_tile(i):
            if i < TC:
                return prob[:, i * CH:(i + 1) * CH]
            at = TC * CH + (i - TC) * S
            return prob[:, at:at + S]

        ffn = ctxT[:, :, :, :].rearrange("p a r s -> p (a r s)")
        wb_parts = ffn[:, 0:2 * KT * HID].rearrange("p (a k n) -> p a k n", a=2, k=KT)
        at = 2 * KT * HID
        wg_parts = ffn[:, at:at + 2 * KT * NGATE].rearrange("p (a k n) -> p a k n", a=2, k=KT)
        at += 2 * KT * NGATE
        ba_parts = ffn[:, at:at + 2 * HID].rearrange("p (a n) -> p a n", a=2)
        gated_parts = v[:, :, 0, :]
        wb_raw = prob[:, 0:KT * HID].rearrange("p (k n) -> p k n", k=KT)
        at = KT * HID
        wg_raw = prob[:, at:at + KT * NGATE].rearrange("p (k n) -> p k n", k=KT)
        at += KT * NGATE
        ba_raw = prob[:, at:at + HID]
        at += HID
        ffn_weights = ((wg_parts, wg_raw),
                       (wb_parts[:, :, 0:KT // 2, :], wb_raw[:, 0:KT // 2, :]),
                       (wb_parts[:, :, KT // 2:, :], wb_raw[:, KT // 2:, :]),
                       (ba_parts, ba_raw))
        bias_sum = prob[:, at:at + HID]
        bias_o = prob[:, at + HID:at + 2 * HID]
        at += 2 * HID
        xn = prob[:, at:at + 2 * HID].rearrange("p (a n) -> p a n", a=2)
        gated = vT[:, 0:2 * P].rearrange("p (a n) -> p a n", a=2)

        scores = ctx.enter_context(nc.psum_tensor("scores", [P, 4, CH], f32))
        turned = ctx.enter_context(nc.psum_tensor("turned", [P, LAG, CH], f32))
        attended = ctx.enter_context(nc.psum_tensor("attended", [P, CH], f32))
        shared = ctx.enter_context(nc.psum_tensor("shared", [P, CH], f32))

        def score_parts(i):
            n = (i + 1) * P
            if i < TC:
                return [(0, n, scores[:, i, 0:n])]
            b = 2 * (i % 2)
            cut = n // 2 if i == TC else CH
            return [(0, cut, scores[:, b, 0:cut]), (cut, n, scores[:, b + 1, 0:n - cut])]

        def tile_scores(i):
            if i < TC:
                return scores[:, i, 0:(i + 1) * P]
            b = 2 * (i % 2)
            if i == TC:
                return scores[:, b:b + 2, 0:(i + 1) * P // 2]
            return scores[:, b:b + 2, :].rearrange("p b n -> p (b n)")[:, 0:(i + 1) * P]

        def unit_bank(kind, n):
            if (kind, n) in (("proj", 0), ("proj", 2), ("vproj", 0), ("vturn", 0)):
                return attended[:, :]
            return shared[:, :]

        const_in = sem("const_in")
        table_in = sem("table_in")
        loads_over = sem("loads_over")
        const_ok = sem("const_ok")
        zero_ok = sem("zero_ok")
        x_in = [sem(f"x_in{i}") for i in range(len(STAT_GROUPS))]
        wb_in, wg_in, ffn_in = sem("wb_in"), sem("wg_in"), sem("ffn_in")
        ffn_hi = sem("ffn_hi")
        ffn_split = sem("ffn_split")
        bias_ok = sem("bias_ok")
        bias_added = sem("bias_added")
        moments_ready = sem("moments_ready")
        var_ready = sem("var_ready")
        power_ready = sem("power_ready")
        rstd_ready = sem("rstd_ready")
        stat_step = sem("stat_step")
        xn_ready = sem("xn_ready")
        x_turned = sem("x_turned")
        x_hi = sem("x_hi")
        x_lo = sem("x_lo")
        gate_done = sem("gate_done")
        gate_max = sem("gate_max")
        gate_exp = sem("gate_exp")
        gate_step = sem("gate_step")
        weight_step = sem("weight_step")
        gated_ready = sem("gated_ready")
        gated_turned = sem("gated_turned")
        gated_hi = sem("gated_hi")
        gated_lo = sem("gated_lo")
        moe_done = sem("moe_done")
        ffn_added = sem("ffn_added")
        wq_in, wk_in, wv_in, wo_in = sem("wq_in"), sem("wk_in"), sem("wv_in"), sem("wo_in")
        wq_split, wk_split, wv_split, wo_split = (sem("wq_split"), sem("wk_split"),
                                                  sem("wv_split"), sem("wo_split"))
        scored = sem("scored")
        max_ready = sem("max_ready")
        exp_done = sem("exp_done")
        block_turned = sem("block_turned")
        block_hi = sem("block_hi")
        block_lo = sem("block_lo")
        block_used = sem("block_used")
        rinv_ready = sem("rinv_ready")
        rinv_out = sem("rinv_out")
        rinv_in = sem("rinv_in")
        ctx_normed = sem("ctx_normed")
        ctx_hi = sem("ctx_hi")
        ctx_lo = sem("ctx_lo")
        proj_done = sem("proj_done")
        proj_biased = sem("proj_biased")
        bias_moved = sem("bias_moved")
        proj_cos = sem("proj_cos")
        proj_sin = sem("proj_sin")
        proj_rotated = sem("proj_rotated")
        proj_hi = sem("proj_hi")
        proj_lo = sem("proj_lo")
        v_done = sem("v_done")
        v_biased = sem("v_biased")
        v_turned = sem("v_turned")
        v_hi = sem("v_hi")
        v_lo = sem("v_lo")
        out_done = sem("out_done")
        out_added = sem("out_added")
        stored = [sem(f"stored{i}") for i in range(2)]

        def tile_no(G, r, i):
            return G * (RH * ST) + (r * ST + i)

        def slot_no(G, r, s):
            return G * (RH * SLOTS) + (r * SLOTS + s)

        def chunk_no(G, r, c):
            return G * (2 * RH) + (2 * r + c)

        def head_no(G, r):
            return G * RH + r

        def unit_no(G, j):
            return G * UNITS + j

        def v_no(G, k):
            return G * 2 + k

        def out_no(G, p, t):
            return G * (2 * ST) + (p * ST + t)

        def wait_shared_bank(eng, G, unit):
            kind = unit[0]
            if kind == "proj":
                eng.wait_ge(proj_biased, unit_no(G, unit[1]) + 1)
            elif kind == "vproj":
                eng.wait_ge(v_biased, v_no(G, unit[1]) + 1)
            elif kind == "vturn":
                eng.wait_ge(v_lo, v_no(G, unit[1]) + 1)
            else:
                eng.wait_ge(out_added, out_no(G, unit[1], unit[2]) + 1)

        block = ctx.enter_context(nc.Block())

        @block.sync
        def _(sp):
            sp.dma_start(ident[:, :], tables[:, 2 * S:2 * S + P]).then_inc(const_in, 16)
            sp.dma_start(mask[:, :], tables[:, 2 * S + P:2 * S + 2 * P]).then_inc(const_in, 16)
            sp.dma_start(bthr_wide[:, :], bthr.partition_broadcast(P)).then_inc(const_in, 16)

            def load_q(g, G, r, first=False):
                if not first:
                    sp.wait_ge(wq_split, head_no(G, r) * 2)
                sp.dma_start(wq_raw[:, :, :], wq[bass.ds(g * RH + r, 1), :, :, :]
                             .rearrange("o p k d -> (o p) k d")).then_inc(wq_in, 16)

            def load_k(g, G, ahead):
                if ahead:
                    sp.wait_ge(wk_split, (G + ahead) * 2)
                sp.dma_start(wk_raw[:, :, :], wk[bass.ds(g + ahead, 1), :, :, :]
                             .rearrange("o p k d -> (o p) k d")).then_inc(wk_in, 16)

            def load_v(g, G, ahead):
                if ahead:
                    sp.wait_ge(wv_split, (G + ahead) * 2)
                sp.dma_start(wv_raw[:, :, :], wv[bass.ds(g + ahead, 1), :, :, :]
                             .rearrange("o p k d -> (o p) k d")).then_inc(wv_in, 16)

            def load_o(g, G, p, first=False):
                if not first:
                    sp.wait_ge(wo_split, (G * 2 + p) * 2)
                sp.dma_start(wo_raw[:, :, :], wo[bass.ds(g * RH + 2 * p, 2), :, :]
                             .rearrange("h d n -> d h n")).then_inc(wo_in, 16)

            def load_x(b, t):
                sp.dma_start(acc[:, t, :], x[bass.ds(b, 1), t * P:(t + 1) * P, :]
                             .rearrange("o p n -> (o p) n")).then_inc(x_in[stat_group(t)], 16)

            def spread_rinv(G, r, c):
                n = chunk_no(G, r, c)
                sp.wait_ge(rinv_ready, n + 1)
                sp.dma_start(rinv_row[c, :, :], rinv[:, c * TC:(c + 1) * TC]).then_inc(rinv_out, 16)
                sp.wait_ge(rinv_out, G * (2 * RH * 16) + (2 * r + c + 1) * 16)
                sp.dma_start(rinv_wide[:, c, :], rinv_row[c, :, :].rearrange("p t -> (p t)")
                             .partition_broadcast(P)).then_inc(rinv_in, 16)

            sp.sem_inc(stored[1], 1)
            with sp.Fori(0, B) as b:
                for t in range(TC):
                    load_x(b, t)
                sp.dma_start(wg_raw, wgate).then_inc(wg_in, 16)
                sp.dma_start(wb_raw, wbase).then_inc(wb_in, 16)
                sp.wait_ge(stored[1], b * (TC * 16) + 1)
                for t in range(TC, ST):
                    load_x(b, t)
                sp.dma_start(ba_raw, badapt).then_inc(ffn_in, 16)
                sp.dma_start(bias_sum, bbase.partition_broadcast(P)).then_inc(ffn_in, 16)
                sp.dma_start(bias_o, bo.partition_broadcast(P)).then_inc(ffn_in, 16)
                G0 = b * GROUPS
                load_k(0, G0, 0)
                load_v(0, G0, 0)
                load_q(0, G0, 0, True)
                load_q(0, G0, 1)

                def group(g, G, has_prev, has_next):
                    load_q(g, G, 2)
                    if has_next:
                        load_v(g, G, 1)
                    load_o(g, G, 0, not has_prev)
                    for r in range(RH):
                        spread_rinv(G, r, 0)
                        spread_rinv(G, r, 1)
                        if r == 1:
                            load_o(g, G, 1)
                            if has_next:
                                load_k(g, G, 1)
                        if r == 0 or r < RH - 1 and has_next:
                            load_q(g, G, r + 3)

                group(0, G0, False, True)
                with sp.Fori(1, GROUPS - 1) as g:
                    group(g, b * GROUPS + g, True, True)
                last = GROUPS - 1
                group(last, G0 + last, True, False)
                for t in range(TC):
                    sp.wait_ge(out_added, out_no(G0 + last, 1, t) + 1)
                    sp.dma_start(out[bass.ds(b, 1), t * P:(t + 1) * P, :]
                                 .rearrange("o p n -> (o p) n"), acc[:, t, :])\
                      .then_inc(stored[0], 16)
                sp.wait_ge(stored[0], b * (TC * 16) + TC * 16)
                sp.sem_inc(loads_over, 1)
            sp.wait_ge(stored[1], B * TC * 16 + 1)

        @block.gpsimd
        def _(pool):
            def split(hi, lo, raw, done, count):
                zeros = zero[:, 0:1]
                for _ in raw.shape[2:]:
                    zeros = zeros.unsqueeze(2)
                pool.tensor_tensor(hi, raw, zeros.to_broadcast(list(raw.shape)), ALU.add)\
                    .then_inc(done, 1)
                pool.wait_ge(done, count + 1)
                pool.tensor_tensor(lo, raw, hi.bitcast(f32), ALU.subtract).then_inc(done, 1)

            def split_q(G, r):
                pool.wait_ge(wq_in, (head_no(G, r) + 1) * 16)
                ahead, r4 = divmod(r, RH)
                if r:
                    pool.wait_ge(proj_done, unit_no(G, UNITS * ahead + (2 + 2 * r4 if r4 else 0)))
                split(wq_parts[:, HI, :, :], wq_parts[:, LO, :, :], wq_raw[:, :, :],
                      wq_split, head_no(G, r) * 2)

            def split_k(G, ahead):
                pool.wait_ge(wk_in, (G + (ahead + 1)) * 16)
                if ahead:
                    pool.wait_ge(proj_done, unit_no(G, 3))
                split(wk_parts[:, HI, :, :], wk_parts[:, LO, :, :], wk_raw[:, :, :],
                      wk_split, (G + ahead) * 2)

            def split_v(G, ahead):
                pool.wait_ge(wv_in, (G + (ahead + 1)) * 16)
                if ahead:
                    pool.wait_ge(v_done, v_no(G, 2))
                split(wv_parts[:, HI, :, :], wv_parts[:, LO, :, :], wv_raw[:, :, :],
                      wv_split, (G + ahead) * 2)

            def split_o(G, p, has_prev):
                pool.wait_ge(wo_in, (G * 2 + (p + 1)) * 16)
                if has_prev:
                    pool.wait_ge(out_done, out_no(G, p - 1, 0))
                split(wo_parts[:, p, HI, :, :], wo_parts[:, p, LO, :, :], wo_raw[:, :, :],
                      wo_split, (G * 2 + p) * 2)

            def rotate(G, j):
                n, a = unit_no(G, j), j % 2
                c = proj_target(j)[1]
                pool.wait_ge(proj_biased, n + 1)
                if j >= 2:
                    pool.wait_ge(proj_lo, unit_no(G, j - 1))
                pool.tensor_tensor(rotated[:, a, :], biased[:, a, :],
                                   cos_sin[:, 0, c * CH:(c + 1) * CH], ALU.mult)\
                    .then_inc(proj_cos, 1)

            def rotated_low(G, j):
                what, c, _ = proj_target(j)
                to = (qT if what == "q" else kT)[:, :, c * CH:(c + 1) * CH]
                pool.wait_ge(proj_hi, unit_no(G, j) + 1)
                pool.tensor_tensor(to[:, LO, :], rotated[:, j % 2, :], to[:, HI, :].bitcast(f32),
                                   ALU.subtract).then_inc(proj_lo, 1)

            def ctx_low(G, r, c):
                to = ctxT[:, :, r % RH, c * CH:(c + 1) * CH]
                pool.wait_ge(ctx_hi, chunk_no(G, r, c) + 1)
                pool.tensor_tensor(to[:, LO, :], normed[:, :], to[:, HI, :].bitcast(f32),
                                   ALU.subtract).then_inc(ctx_lo, 1)

            def group(G, has_prev, has_next):
                for r in range(RH):
                    for s in range(SLOTS):
                        if s == 2 and (r or has_prev):
                            ctx_low(G, r - 1, 1)
                        if s == 6:
                            ctx_low(G, r, 0)
                        for u in units_cut(r, s, has_prev, has_next):
                            rotated_low(G, u[1])
                        for u in units_of(r, s, has_prev, has_next):
                            if u[0] == "proj":
                                rotate(G, u[1])
                        if s == 9 and (r < 2 or has_next):
                            split_q(G, r + 2)
                        if s == 10 and r == 0 and has_next:
                            split_v(G, 1)
                        if s == 3 and r == 1:
                            split_o(G, 0, has_prev)
                        if s == 10 and r == 2 and has_next:
                            split_k(G, 1)
                        if s == 6 and r == 2:
                            split_o(G, 1, has_prev)

            pool.memset(zero[:, :], 0.0).then_inc(zero_ok, 1)
            pool.memset(minus_half[:, :], -0.5).then_inc(zero_ok, 1)
            pool.wait_ge(zero_ok, 2)
            with pool.Fori(0, B) as b:
                def power(n):
                    tiles = slice(*STAT_GROUPS[n])
                    pool.wait_ge(var_ready, b * len(STAT_GROUPS) + (n + 1))
                    pool.tensor_tensor(rstd[:, 1, tiles], rstd[:, 0, tiles],
                                       minus_half[:, tiles], ALU.pow).then_inc(power_ready, 1)

                power(0)
                for n, (parts, raw) in enumerate(ffn_weights):
                    if n == 1:
                        power(1)
                    pool.wait_ge(ffn_hi, b * len(ffn_weights) + (n + 1))
                    pool.tensor_tensor(parts[:, LO], raw, parts[:, HI].bitcast(f32),
                                       ALU.subtract).then_inc(ffn_split, 1)
                pool.tensor_tensor(bias_sum, bias_sum, bias_o, ALU.add).then_inc(bias_ok, 1)
                pool.wait_ge(bias_ok, b + 1)
                G0 = b * GROUPS
                for t in range(ST):
                    pool.wait_ge(xn_ready, b * ST + (t + 1))
                    pool.tensor_tensor(acc[:, t, :], acc[:, t, :], bias_sum, ALU.add)\
                        .then_inc(bias_added, 1)
                    if t == TC - 1:
                        power(2)
                    if t == TC:
                        split_k(G0, 0)
                        split_q(G0, 0)
                        split_v(G0, 0)
                pool.wait_ge(table_in, 16 * 2)
                rotate(G0, 0)
                for j in range(PRE_UNITS):
                    if j + 1 < PRE_UNITS:
                        rotate(G0, j + 1)
                    rotated_low(G0, j)
                split_q(G0, 1)
                group(G0, False, True)
                with pool.Fori(1, GROUPS - 1) as g:
                    group(b * GROUPS + g, True, True)
                group(G0 + (GROUPS - 1), True, False)
                ctx_low(G0 + (GROUPS - 1), RH - 1, 1)
                pool.wait_ge(out_done, b * (2 * GROUPS * ST) + 2 * GROUPS * ST)

        @block.scalar
        def _(act):
            def copy(to, source):
                return act.activation(to, source, ACT.Copy)

            def exponentials(G, r, i, first):
                n = (i + 1) * P
                c = i // TC
                act.wait_ge(max_ready, tile_no(G, r, i) + 1)
                if not first:
                    act.wait_ge(block_turned, slot_no(G, r - 1, i if c == 0 else TC + i) + 1)
                    if i % TC == 0:
                        act.wait_ge(rinv_ready, chunk_no(G, r - 1, c) + 1)
                to = prob_tile(i)[:, 0:n]
                if i == TC:
                    to = to.rearrange("p (b n) -> p b n", b=2)
                act.activation(to, tile_scores(i), ACT.Exp,
                               bias=neg_max[:, i:i + 1], accum_out=row_sum[:, i:i + 1])\
                   .then_inc(exp_done, 1)

            def block_high(G, r, s, first):
                a, at = s % 2, block_start(s)
                act.wait_ge(block_turned, slot_no(G, r, s) + 1)
                if not first or s >= LAG:
                    act.wait_ge(block_used, slot_no(G, r, s - LAG) + 1)
                copy(probT[:, a, HI, at:CH], turned[:, a, at:CH]).then_inc(block_hi, 1)

            def projected(G, j):
                what, _, r = proj_target(j)
                if j < PRE_UNITS:
                    column = bias[:, GROUPS * NB + (what == "k"):GROUPS * NB + 1 + (what == "k")]
                else:
                    column = bias_now[:, r - 1:r] if what == "q" else bias_now[:, RH:RH + 1]
                    act.wait_ge(bias_moved, G + 1)
                act.wait_ge(proj_done, unit_no(G, j) + 1)
                if j >= 2:
                    act.wait_ge(proj_cos, unit_no(G, j - 1))
                    act.wait_ge(proj_sin, unit_no(G, j - 1) * 2)
                act.activation(biased[:, j % 2, :], unit_bank("proj", j), ACT.Identity,
                               bias=column).then_inc(proj_biased, 1)

            def rotated_high(G, j):
                what, c, r = proj_target(j)
                to = (qT if what == "q" else kT)[:, HI, c * CH:(c + 1) * CH]
                act.wait_ge(proj_rotated, unit_no(G, j) + 1)
                if j >= PRE_UNITS:
                    i = TC - 1 if what == "q" and c == 0 else ST - 1
                    act.wait_ge(scored, tile_no(G, r - 1, i) + 1)
                copy(to, rotated[:, j % 2, :]).then_inc(proj_hi, 1)

            def v_projected(G, k):
                c = k % 2
                act.wait_ge(v_done, v_no(G, k) + 1)
                if k >= 2:
                    act.wait_ge(v_turned, v_no(G, k - 2) + 1)
                column = bias_now[:, RH + 1:RH + 2] if k >= 2 else bias[:, GROUPS * NB + 2:]
                act.activation(vT[:, c * CH:(c + 1) * CH], unit_bank("vproj", k), ACT.Identity,
                               bias=column).then_inc(v_biased, 1)

            def move_bias(g):
                copy(bias_now[:, :], bias[:, bass.ds(g * NB, NB)]).then_inc(bias_moved, 1)

            def v_high(G, k, has_prev):
                u = k % 2
                act.wait_ge(v_turned, v_no(G, k) + 1)
                if k > 1 or has_prev:
                    act.wait_ge(block_used, slot_no(G, (k // 2) * RH - 1, TC + TC * u + TC - 1) + 1)
                copy(v[:, HI, TC * u:TC * (u + 1), :].rearrange("p t d -> p (t d)"),
                     unit_bank("vturn", k)).then_inc(v_hi, 1)

            def ctx_high(G, r, c, has_prev):
                act.wait_ge(ctx_normed, chunk_no(G, r, c) + 1)
                if c == 0 and r % 2 == 0 and has_prev:
                    act.wait_ge(out_done, out_no(G, r // 2 - 1, 0))
                copy(ctxT[:, HI, r % RH, c * CH:(c + 1) * CH], normed[:, :]).then_inc(ctx_hi, 1)

            def group(G, g, has_prev, has_next):
                for r in range(RH):
                    first = not r and not has_prev
                    for s in range(SLOTS):
                        if s != 2:
                            block_high(G, r, s, first)
                        if s == 0:
                            if not first:
                                exponentials(G, r, TC, first)
                        elif score_tile(s - 1) is not None and s != 3:
                            ahead, i = score_tile(s - 1)
                            if not ahead or r < RH - 1 or has_next:
                                exponentials(G, r + ahead, i, first and not ahead)
                        if s == 2:
                            block_high(G, r, s, first)
                            exponentials(G, r, TC + 3, first)
                        if s == 6:
                            ctx_high(G, r, 0, has_prev)
                        for u in units_of(r, s, has_prev, has_next):
                            if u[0] == "proj":
                                projected(G, u[1])
                            if u[0] == "vproj":
                                v_projected(G, u[1])
                            if u[0] == "vturn":
                                v_high(G, u[1], has_prev)
                        if s == 2 and not first:
                            ctx_high(G, r - 1, 1, has_prev)
                        for u in units_cut(r, s, has_prev, has_next):
                            rotated_high(G, u[1])
                        if r == RH - 1 and s == SLOTS - 2 and has_next:
                            move_bias(g + 1)

            act.wait_ge(x_in[1], (TC - 1) * 16)
            act.dma_start(cos_sin[:, :, :], tables[:, 0:2 * S].rearrange("p (a s) -> p a s", a=2))\
               .then_inc(table_in, 16)
            act.dma_start(bias[:, :], bqkv).then_inc(table_in, 16)
            with act.Fori(0, B) as b:
                def weights_high(n):
                    parts, raw = ffn_weights[n]
                    copy(parts[:, HI], raw).then_inc(ffn_hi, 1)

                act.wait_ge(wg_in, b * 16 + 16)
                weights_high(0)
                for k in range(ST + 2):
                    T = b * ST + k
                    if k < ST:
                        act.wait_ge(x_turned, T + 1)
                        copy(xnT[:, HI, :, k * P:(k + 1) * P],
                             turned[:, k % 2, :].rearrange("p (k s) -> p k s", k=KT))\
                            .then_inc(x_hi, 1)
                    if k == 0:
                        act.wait_ge(wb_in, b * 16 + 16)
                        weights_high(1)
                        weights_high(2)
                    if k == 1:
                        act.wait_ge(ffn_in, b * (16 * 3) + 16 * 3)
                        weights_high(3)
                    if k >= 2:
                        act.wait_ge(gated_turned, T - 1)
                        if k > 2:
                            act.wait_ge(moe_done, T - 2)
                        copy(gated_parts[:, HI, :], shared[:, 0:P]).then_inc(gated_hi, 1)
                    if 1 <= k <= ST:
                        bank = scores[:, 2 + (k - 1) % 2, :]
                        act.wait_ge(gate_max, T)
                        act.activation(gate[:, 0, :], bank[:, E * R:E * R + E], ACT.Exp,
                                       bias=thr[:, 0:1], accum_out=thr[:, 1:2])\
                           .then_inc(gate_exp, 1)
                        act.activation(thr[:, 2:3], bank[:, E * R + E:E * R + E + 1], ACT.Exp,
                                       bias=neg_bthr[:, 0:1], scale=-1.0).then_inc(gate_exp, 1)
                G0 = b * GROUPS
                act.wait_ge(table_in, 16 * 2)
                projected(G0, 0)
                projected(G0, 1)
                rotated_high(G0, 0)
                projected(G0, 2)
                rotated_high(G0, 1)
                projected(G0, 3)
                rotated_high(G0, 2)
                v_projected(G0, 0)
                rotated_high(G0, 3)
                for i in range(TC):
                    exponentials(G0, 0, i, True)
                v_projected(G0, 1)
                move_bias(0)
                v_high(G0, 0, False)
                exponentials(G0, 0, TC, True)
                group(G0, 0, False, True)
                with act.Fori(1, GROUPS - 1) as g:
                    group(b * GROUPS + g, g, True, True)
                group(G0 + (GROUPS - 1), GROUPS - 1, True, False)
                ctx_high(G0 + (GROUPS - 1), RH - 1, 1, True)
                for t in range(TC, ST):
                    act.wait_ge(out_added, out_no(G0 + (GROUPS - 1), 1, t) + 1)
                    act.dma_start(out[bass.ds(b, 1), t * P:(t + 1) * P, :]
                                  .rearrange("o p n -> (o p) n"), acc[:, t, :])\
                       .then_inc(stored[1], 16)

        @block.vector
        def _(dve):
            def row_max(G, r, i):
                dve.wait_ge(scored, tile_no(G, r, i) + 1)
                dve.reduce_max(neg_max[:, i:i + 1], tile_scores(i), AX.XY if i == TC else AX.X,
                               negate=True).then_inc(max_ready, 1)

            def inverse(G, r, c, first):
                dve.wait_ge(exp_done, tile_no(G, r, TC * c + TC - 1) + 1)
                if not first:
                    dve.wait_ge(ctx_normed, chunk_no(G, r - 1, c) + 1)
                dve.reciprocal(rinv[:, TC * c:TC * c + TC], row_sum[:, TC * c:TC * c + TC])\
                   .then_inc(rinv_ready, 1)

            def block_low(G, r, s):
                a, at = s % 2, block_start(s)
                dve.wait_ge(block_hi, slot_no(G, r, s) + 1)
                dve.tensor_tensor(probT[:, a, LO, at:CH], turned[:, a, at:CH],
                                  probT[:, a, HI, at:CH].bitcast(f32), ALU.subtract)\
                   .then_inc(block_lo, 1)

            def cross(G, j):
                n, a = unit_no(G, j), j % 2
                c = proj_target(j)[1]
                half = D // 2
                dve.wait_ge(proj_biased, n + 1)
                if j >= 2:
                    dve.wait_ge(proj_rotated, unit_no(G, j - 1))
                for to, of in ((0, half), (half, 0)):
                    dve.tensor_tensor(crossed[to:to + half, a, :], biased[of:of + half, a, :],
                                      cos_sin[of:of + half, 1, c * CH:(c + 1) * CH], ALU.mult)\
                       .then_inc(proj_sin, 1)

            def rotate(G, j):
                n, a = unit_no(G, j), j % 2
                dve.wait_ge(proj_cos, n + 1)
                dve.wait_ge(proj_sin, n * 2 + 2)
                dve.tensor_tensor(rotated[:, a, :], rotated[:, a, :], crossed[:, a, :], ALU.add)\
                   .then_inc(proj_rotated, 1)

            def v_low(G, k):
                u = k % 2
                dve.wait_ge(v_hi, v_no(G, k) + 1)
                to = v[:, :, TC * u:TC * (u + 1), :].rearrange("p a t d -> p a (t d)")
                dve.tensor_tensor(to[:, LO, :], unit_bank("vturn", k), to[:, HI, :].bitcast(f32),
                                  ALU.subtract).then_inc(v_lo, 1)

            def normalise(G, r, c, first=False):
                n = chunk_no(G, r, c)
                dve.wait_ge(block_used, slot_no(G, r, TC - 1 if c == 0 else SLOTS - 1) + 1)
                dve.wait_ge(rinv_in, (n + 1) * 16)
                if not first:
                    dve.wait_ge(ctx_lo, n)
                dve.tensor_tensor(normed[:, :].rearrange("p (t q) -> p t q", t=TC),
                                  attended[:, :].rearrange("p (t q) -> p t q", t=TC),
                                  rinv_wide[:, c, :].rearrange("p (q t) -> p t q", t=TC),
                                  ALU.mult)\
                   .then_inc(ctx_normed, 1)

            def add_out(G, p, t, bank=shared[:, :]):
                dve.wait_ge(out_done, out_no(G, p, t) + 1)
                dve.wait_ge(out_added, out_no(G, p - 1, t) + 1)
                dve.tensor_tensor(acc[:, t, :], acc[:, t, :], bank, ALU.add)\
                   .then_inc(out_added, 1)

            def add_out_first(G, t):
                dve.wait_ge(out_done, out_no(G, 0, t) + 1)
                dve.tensor_tensor(acc[:, t, :], acc[:, t, :], shared[:, :], ALU.add)\
                   .then_inc(out_added, 1)

            def group(G, has_prev, has_next):
                for r in range(RH):
                    first = not r and not has_prev
                    for s in range(SLOTS):
                        if s in (0, 4):
                            inverse(G, r, s // TC, first)
                        if s == 1 and not first:
                            normalise(G, r - 1, 1)
                        if s == 5:
                            normalise(G, r, 0, first)
                        if s == 2:
                            row_max(G, r, TC + 3)
                        block_low(G, r, s)
                        for u in units_of(r, s - 2, has_prev, has_next):
                            if u[0] == "proj":
                                rotate(G, u[1])
                        if score_tile(s) is not None and s != 2:
                            ahead, i = score_tile(s)
                            if not ahead or r < RH - 1 or has_next:
                                row_max(G, r + ahead, i)
                        for u in units_of(r, s - 1, has_prev, has_next):
                            if u[0] == "proj":
                                cross(G, u[1])
                        for u in units_of(r, s, has_prev, has_next):
                            if u[0] == "vturn":
                                v_low(G, u[1])
                            if u[0] == "out":
                                if has_prev:
                                    add_out(G, u[1], u[2])
                                else:
                                    add_out_first(G, u[2])

            dve.wait_ge(const_in, 16 * 3)
            dve.tensor_copy(ident_b[:, :], ident[:, :]).then_inc(const_ok, 1)
            dve.tensor_copy(mask_b[:, :], mask[:, :]).then_inc(const_ok, 1)
            dve.tensor_scalar(neg_bthr[:, 0:1], bthr_wide[:, :], -1.0, None, ALU.mult)\
               .then_inc(const_ok, 1)
            with dve.Fori(0, B) as b:
                def chained(instruction, done, count):
                    instruction.then_inc(done, 1)
                    dve.wait_ge(done, count)

                def moments_of(t):
                    start, end = STAT_GROUPS[stat_group(t)]
                    if t == start:
                        n = (end - start) * 16
                        dve.wait_ge(x_in[stat_group(t)], b * n + n)
                    dve.bn_stats(stats[:, t, :], acc[:, t, :]).then_inc(moments_ready, 1)

                def inverse_std(n):
                    def step(instruction, k):
                        chained(instruction, stat_step, b * (4 * len(STAT_GROUPS)) + (4 * n + k))
                    start, end = STAT_GROUPS[n]
                    tiles = slice(start, end)
                    dve.wait_ge(moments_ready, b * ST + end)
                    even, odd = stats[:, tiles, 0:3], stats[:, tiles, 3:6]
                    dve.tensor_tensor(moments[:, 0, tiles], even[:, :, 1], odd[:, :, 1], ALU.add)
                    dve.tensor_tensor(moments[:, 1, tiles], even[:, :, 1], odd[:, :, 1],
                                      ALU.subtract)
                    step(dve.tensor_tensor(moments[:, 2, tiles], even[:, :, 2], odd[:, :, 2],
                                           ALU.add), 1)
                    dve.tensor_scalar(moments[:, 3, tiles], moments[:, 0, tiles], 0.5, None,
                                      ALU.mult)
                    dve.tensor_tensor(moments[:, 4, tiles], moments[:, 1, tiles],
                                      moments[:, 1, tiles], ALU.mult)
                    step(dve.tensor_scalar(moments[:, 5, tiles], moments[:, 2, tiles],
                                           1.0 / HID, EPS, ALU.mult, ALU.add), 2)
                    count = b * len(STAT_GROUPS) + (n + 1)
                    chained(dve.scalar_tensor_tensor(rstd[:, 0, tiles], moments[:, 4, tiles],
                                                     0.25, moments[:, 5, tiles],
                                                     ALU.mult, ALU.add), var_ready, count)
                    dve.tensor_scalar(rstd[:, 3, tiles], rstd[:, 0, tiles], -0.5, None, ALU.mult)
                    dve.wait_ge(power_ready, count)
                    step(dve.tensor_tensor(rstd[:, 4, tiles], rstd[:, 1, tiles],
                                           rstd[:, 1, tiles], ALU.mult), 3)
                    step(dve.tensor_tensor(rstd[:, 5, tiles], rstd[:, 4, tiles],
                                           rstd[:, 3, tiles], ALU.mult), 4)
                    chained(dve.scalar_tensor_tensor(rstd[:, 2, tiles], rstd[:, 5, tiles], 1.5,
                                                     rstd[:, 1, tiles], ALU.add, ALU.mult),
                            rstd_ready, count)

                def normalised(t):
                    T = b * ST + t
                    if t >= 2:
                        dve.wait_ge(x_turned, T - 1)
                    dve.tensor_scalar(xn[:, t % 2, :], acc[:, t, :], moments[:, 3, t:t + 1],
                                      rstd[:, 2, t:t + 1], ALU.subtract, ALU.mult)\
                       .then_inc(xn_ready, 1)

                def gating(t):
                    T = b * ST + t
                    bank = scores[:, 2 + t % 2, :]

                    def step(instruction, k):
                        chained(instruction, gate_step, T * 7 + k)
                    dve.wait_ge(gate_done, T + 1)
                    dve.reduce_max(thr[:, 0:1], bank[:, E * R:E * R + E], AX.X, negate=True)\
                       .then_inc(gate_max, 1)
                    dve.wait_ge(gate_exp, T * 2 + 2)
                    dve.reciprocal(thr[:, 3:4], thr[:, 1:2])
                    step(dve.tensor_scalar(thr[:, 4:5], thr[:, 2:3], 1.0, None, ALU.add), 1)
                    step(dve.reciprocal(thr[:, 5:6], thr[:, 4:5]), 2)
                    step(dve.tensor_scalar(thr[:, 6:7], thr[:, 5:6], MAX_THR, None, ALU.mult), 3)
                    step(dve.tensor_scalar(gate[:, 1, :], gate[:, 0, :], thr[:, 3:4], thr[:, 6:7],
                                           ALU.mult, ALU.subtract), 4)
                    step(dve.tensor_scalar(gate[:, 2, :], gate[:, 1, :], 0.0, None, ALU.max), 5)
                    step(dve.reduce_sum(thr[:, 7:8], gate[:, 2, :], AX.X), 6)
                    step(dve.scalar_tensor_tensor(thr[:, 8:9], thr[:, 7:8], 0.0, thr[:, 7:8],
                                                  ALU.is_equal, ALU.add), 7)
                    chained(dve.reciprocal(thr[:, 9:10], thr[:, 8:9]), weight_step, T * 2 + 1)
                    chained(dve.tensor_scalar(gate[:, 3, :], gate[:, 2, :], thr[:, 9:10], SCALING,
                                              ALU.mult, ALU.mult), weight_step, T * 2 + 2)
                    if t >= 2:
                        dve.wait_ge(gated_turned, T - 1)
                    dve.tensor_tensor(gated[:, t % 2, :].rearrange("p (e r) -> p e r", e=E),
                                      bank[:, 0:E * R].rearrange("p (e r) -> p e r", e=E),
                                      gate[:, 3, :].unsqueeze(2).to_broadcast([P, E, R]),
                                      ALU.mult).then_inc(gated_ready, 1)

                moments_of(0)
                inverse_std(0)
                normalised(0)
                for t in range(1, TC):
                    moments_of(t)
                for k in range(ST + 2):
                    T = b * ST + k
                    if 0 < k < ST - 1:
                        normalised(k + 1)
                    if k < ST:
                        dve.wait_ge(x_hi, T + 1)
                        part = xnT[:, :, :, k * P:(k + 1) * P]
                        dve.tensor_tensor(part[:, LO, :, :],
                                          turned[:, k % 2, :].rearrange("p (k s) -> p k s", k=KT),
                                          part[:, HI, :, :].bitcast(f32), ALU.subtract)\
                           .then_inc(x_lo, 1)
                    if k == 0:
                        inverse_std(1)
                        normalised(1)
                    if k >= 2:
                        dve.wait_ge(gated_hi, T - 1)
                        dve.tensor_tensor(gated_parts[:, LO, :], shared[:, 0:P],
                                          gated_parts[:, HI, :].bitcast(f32), ALU.subtract)\
                           .then_inc(gated_lo, 1)
                    if 1 <= k <= ST:
                        gating(k - 1)
                    if k >= 2:
                        t = k - 2
                        dve.wait_ge(moe_done, T - 1)
                        dve.wait_ge(bias_added, T - 1)
                        dve.tensor_tensor(acc[:, t, :], acc[:, t, :], scores[:, t % 2, :], ALU.add)\
                           .then_inc(ffn_added, 1)
                    if k in (1, 2):
                        moments_of(TC + 2 * (k - 1))
                        moments_of(TC + 2 * (k - 1) + 1)
                    if k == 2:
                        inverse_std(2)
                G0 = b * GROUPS
                dve.wait_ge(table_in, 16 * 2)
                cross(G0, 0)
                for j in range(PRE_UNITS):
                    if j + 1 < PRE_UNITS:
                        cross(G0, j + 1)
                    rotate(G0, j)
                for i in range(TC):
                    row_max(G0, 0, i)
                v_low(G0, 0)
                row_max(G0, 0, TC)
                dve.wait_ge(ffn_added, b * ST + ST)
                group(G0, False, True)
                with dve.Fori(1, GROUPS - 1) as g:
                    group(b * GROUPS + g, True, True)
                last = G0 + (GROUPS - 1)
                group(last, True, False)
                normalise(last, RH - 1, 1)
                for t in range(TC, ST):
                    add_out(last, 1, t, scores[:, t % TC, :])

        @block.tensor
        def _(pe):
            def product(to, lhs, rhs, first=True, last=True):
                for n, (a, c) in enumerate(((HI, HI), (HI, LO), (LO, HI))):
                    mm = pe.matmul(to, lhs[a], rhs[c], start=first and n == 0,
                                   stop=last and n == 2)
                return mm

            def parts(t, *at):
                return t[(slice(None), HI, *at)], t[(slice(None), LO, *at)]

            def score(G, r, i, first):
                c = i // TC
                if i % TC == 0:
                    ahead, r4 = divmod(r, RH)
                    j = UNITS * ahead + (1 + 2 * c if r4 == 0 else 2 + 2 * r4 + c)
                    pe.wait_ge(proj_lo, unit_no(G, j) + 1)
                if c == 0 and not first:
                    pe.wait_ge(exp_done, tile_no(G, r - 1, 6 + i // 2) + 1)
                if c == 1:
                    pe.wait_ge(exp_done, tile_no(G, r, (1, 3, 4, 5)[i - TC]) + 1)
                q = parts(qT, slice(i * P, (i + 1) * P))
                for at, to, bank in score_parts(i):
                    diagonal = to == (i + 1) * P
                    mm = product(bank, q, parts(kT, slice(at, to)), last=not diagonal)
                    if diagonal:
                        mm = pe.matmul(bank[:, to - at - P:to - at], ident_b[:, :], mask_b[:, :],
                                       start=False, stop=True)
                mm.then_inc(scored, 1)

            def turn_block(G, r, s, first):
                c, j = chunk_block(s)
                if s in (0, TC):
                    pe.wait_ge(exp_done, tile_no(G, r, TC * c + TC - 1) + 1)
                if not first or s >= LAG:
                    pe.wait_ge(block_lo, slot_no(G, r, s - LAG) + 1)
                for i in range(block_start(s) // P, TC):
                    mm = pe.matmul(turned[:, s % 2, i * P:(i + 1) * P],
                                   prob_tile(TC * c + i)[:, j * P:(j + 1) * P], ident[:, :],
                                   is_transpose=True)
                mm.then_inc(block_turned, 1)

            def attend(G, r, s, first):
                c, j = chunk_block(s)
                if j == 0 and not (first and c == 0):
                    pe.wait_ge(ctx_normed, chunk_no(G, r, c))
                if r == 0 and s in (0, TC + TC):
                    pe.wait_ge(v_lo, v_no(G, s // (2 * TC)) + 1)
                pe.wait_ge(block_lo, slot_no(G, r, s) + 1)
                at = block_start(s)
                product(attended[:, at:CH], parts(v, j),
                        (probT[:, s % 2, HI, at:CH], probT[:, s % 2, LO, at:CH]),
                        first=j == 0, last=j == TC * c + TC - 1).then_inc(block_used, 1)

            def project(G, j):
                what, c, r = proj_target(j)
                bank = unit_bank("proj", j)
                if what == "q":
                    pe.wait_ge(wq_split, head_no(G, r) * 2 + 2)
                    w = wq_parts
                else:
                    pe.wait_ge(wk_split, (G + r // RH) * 2 + 2)
                    w = wk_parts
                for k in range(KT):
                    mm = product(bank, parts(w, k),
                                 parts(xnT, k, slice(c * CH, (c + 1) * CH)),
                                 first=k == 0, last=k == KT - 1)
                mm.then_inc(proj_done, 1)

            def project_v(G, k):
                c = k % 2
                bank = unit_bank("vproj", k)
                pe.wait_ge(wv_split, (G + k // 2) * 2 + 2)
                for b in range(KT):
                    mm = product(bank, parts(wv_parts, b),
                                 parts(xnT, b, slice(c * CH, (c + 1) * CH)),
                                 first=b == 0, last=b == KT - 1)
                mm.then_inc(v_done, 1)

            def turn_v(G, k):
                u = k % 2
                bank = unit_bank("vturn", k)
                pe.wait_ge(v_biased, v_no(G, k) + 1)
                for i in range(TC):
                    mm = pe.matmul(bank[:, i * P:(i + 1) * P],
                                   vT[:, (TC * u + i) * P:(TC * u + i + 1) * P], ident[:, :],
                                   is_transpose=True)
                mm.then_inc(v_turned, 1)

            def project_out(G, p, t, bank=shared[:, :]):
                pe.wait_ge(ctx_lo, chunk_no(G, 2 * p + 1, t // TC) + 1)
                pe.wait_ge(wo_split, G * 4 + (2 * p + 2))
                for h in range(2):
                    r = (2 * p + h) % RH
                    mm = product(bank, parts(ctxT, r, slice(t * P, (t + 1) * P)),
                                 (wo_parts[:, p % 2, HI, h, :], wo_parts[:, p % 2, LO, h, :]),
                                 first=h == 0, last=h == 1)
                mm.then_inc(out_done, 1)

            def unit(G, u):
                if u[0] == "proj":
                    project(G, u[1])
                elif u[0] == "vproj":
                    project_v(G, u[1])
                elif u[0] == "vturn":
                    turn_v(G, u[1])
                else:
                    project_out(G, u[1], u[2])

            def group(G, has_prev, has_next):
                previous = ("vturn", 0)
                for r in range(RH):
                    first = not r and not has_prev
                    for s in range(SLOTS):
                        turn_block(G, r, s, first)
                        if s == 2:
                            score(G, r, TC + 3, False)
                        if s >= LAG:
                            attend(G, r, s - LAG, first)
                        elif not first:
                            attend(G, r - 1, s - LAG + SLOTS, False)
                        if score_tile(s) is not None and s != 2:
                            ahead, i = score_tile(s)
                            if not ahead or r < RH - 1 or has_next:
                                score(G, r + ahead, i, False)
                        for u in units_of(r, s, has_prev, has_next):
                            wait_shared_bank(pe, G, previous)
                            unit(G, u)
                            previous = u

            def turn_x(b, t):
                T = b * ST + t
                pe.wait_ge(xn_ready, T + 1)
                if t >= 2:
                    pe.wait_ge(x_lo, T - 1)
                for i in range(KT):
                    mm = pe.matmul(turned[:, t % 2, i * P:(i + 1) * P],
                                   xn[:, t % 2, i * P:(i + 1) * P], ident[:, :],
                                   is_transpose=True)
                mm.then_inc(x_turned, 1)

            pe.wait_ge(const_ok, 3)
            with pe.Fori(0, B) as b:
                for k in range(ST + 2):
                    T = b * ST + k
                    if k < ST and k != 1:
                        turn_x(b, k)
                    if k >= 2:
                        pe.wait_ge(gated_ready, T - 1)
                        if k > 2:
                            pe.wait_ge(gated_lo, T - 2)
                        pe.matmul(shared[:, 0:P], gated[:, k % 2, :], ident[:, :],
                                  is_transpose=True).then_inc(gated_turned, 1)
                    if 1 <= k <= ST:
                        t = k - 1
                        if t == 0:
                            pe.wait_ge(ffn_split, b * 4 + 1)
                        pe.wait_ge(x_lo, T)
                        tile = slice(t * P, (t + 1) * P)
                        if t >= 2:
                            pe.wait_ge(gated_ready, T - 2)
                        for i in range(KT):
                            mm = product(scores[:, 2 + t % 2, 0:NGATE], parts(xnT, i, tile),
                                         (wg_parts[:, HI, i, :], wg_parts[:, LO, i, :]),
                                         first=i == 0, last=i == KT - 1)
                        mm.then_inc(gate_done, 1)
                        if k == 1:
                            turn_x(b, 1)
                        if t >= 2:
                            pe.wait_ge(ffn_added, T - 2)
                        for i in range(KT):
                            if t == 0 and i in (0, KT // 2):
                                pe.wait_ge(ffn_split, b * 4 + (2 if i == 0 else 3))
                            product(scores[:, t % 2, :], parts(xnT, i, tile),
                                    (wb_parts[:, HI, i, :], wb_parts[:, LO, i, :]),
                                    first=i == 0, last=False)
                    if k == ST + 1:
                        project(b * GROUPS, 0)
                    if k == 2:
                        pe.wait_ge(ffn_split, b * 4 + 4)
                    if k >= 2:
                        pe.wait_ge(gated_lo, T - 1)
                        product(scores[:, k % 2, :],
                                (gated_parts[:, HI, :], gated_parts[:, LO, :]),
                                (ba_parts[:, HI, :], ba_parts[:, LO, :]),
                                first=False).then_inc(moe_done, 1)
                G0 = b * GROUPS
                for j in range(1, PRE_UNITS):
                    if j >= 2:
                        wait_shared_bank(pe, G0, ("proj", j - 2))
                    project(G0, j)
                wait_shared_bank(pe, G0, ("proj", PRE_UNITS - 2))
                project_v(G0, 0)
                pe.wait_ge(ffn_added, b * ST + ST)
                for i in range(TC):
                    score(G0, 0, i, True)
                wait_shared_bank(pe, G0, ("proj", PRE_UNITS - 1))
                project_v(G0, 1)
                turn_v(G0, 0)
                score(G0, 0, TC, True)
                group(G0, False, True)
                with pe.Fori(1, GROUPS - 1) as g:
                    group(b * GROUPS + g, True, True)
                last = G0 + (GROUPS - 1)
                group(last, True, False)
                for s in (SLOTS - 2, SLOTS - 1):
                    attend(last, RH - 1, s, False)
                for t in range(TC, ST):
                    project_out(last, 1, t, scores[:, t % TC, :])


def position_tables():
    import numpy as np

    half = D // 2
    inv_freq = (1.0 / np.power(np.float32(10000.0),
                               np.arange(half, dtype=np.float32) / np.float32(half))).astype(np.float32)
    angle = (np.arange(S, dtype=np.float32)[None, :] * inv_freq[:, None]).astype(np.float32)
    scale = float(D) ** -0.25
    cos = np.cos(angle.astype(np.float64)) * scale
    sin = np.sin(angle.astype(np.float64)) * scale
    tables = np.zeros((P, 2 * S + 2 * P), np.float32)
    tables[:half, 0:S] = tables[half:, 0:S] = cos
    tables[:half, S:2 * S] = sin
    tables[half:, S:2 * S] = -sin
    tables[:, 2 * S:2 * S + P] = np.eye(P)
    tables[:, 2 * S + P:] = np.where(np.tril(np.ones((P, P), bool)), 0.0, -1e30)
    return tables


def kernel(**inputs):
    import numpy as np
    import concourse.bacc as bacc
    from concourse.bass_utils import run_bass_kernel_spmd

    a = {n: np.asarray(v) for n, v in inputs.items()}

    def by_rows(w, n):
        return w.reshape(KT, P, n, D).transpose(2, 1, 0, 3)

    gate_cols = np.concatenate([a["L0_ffn_A"].reshape(E * R, HID), a["L0_ffn_W_gate"],
                                a["L0_ffn_W_thr"], np.zeros((1, HID), np.float32)]).T
    bq, bk, bv = (a[f"L0_attn_b{n}"].reshape(-1, D) for n in "qkv")
    bias_rows = []
    for g in range(GROUPS):
        n = (g + 1) % GROUPS
        bias_rows += [bq[g * RH + 1], bq[g * RH + 2], bq[g * RH + 3], bq[n * RH], bk[n], bv[n]]
    bias_rows += [bq[0], bk[0], bv[0]]
    arrays = {
        "in_x": a["L0_attn_hidden_states"],
        "in_wq": by_rows(a["L0_attn_Wq"], H),
        "in_wk": by_rows(a["L0_attn_Wk"], GROUPS),
        "in_wv": by_rows(a["L0_attn_Wv"], GROUPS),
        "in_wo": a["L0_attn_Wo"].reshape(H, D, HID),
        "in_bqkv": np.stack(bias_rows).T,
        "in_bo": a["L0_attn_bo"],
        "in_wbase": a["L0_ffn_W_base"].T.reshape(KT, P, HID).transpose(1, 0, 2),
        "in_bbase": a["L0_ffn_b_base"],
        "in_wgate": gate_cols.reshape(KT, P, NGATE).transpose(1, 0, 2),
        "in_bthr": a["L0_ffn_b_thr"],
        "in_badapt": a["L0_ffn_B"].transpose(0, 2, 1).reshape(E * R, HID),
        "in_tables": position_tables(),
    }
    arrays = {n: np.ascontiguousarray(v) for n, v in arrays.items()}
    nc = bacc.Bacc("TRN2", target_bir_lowering=False, num_devices=1)
    f32 = mybir.dt.float32
    args = [nc.dram_tensor(n, v.shape, f32, kind="ExternalInput").ap() for n, v in arrays.items()]
    args.append(nc.dram_tensor("rinv_row", (2, P, TC), f32, kind="Internal").ap())
    args.append(nc.dram_tensor("out", (B, S, HID), f32, kind="ExternalOutput").ap())
    build(nc, *args)
    return run_bass_kernel_spmd(nc, [arrays], core_ids=[0]).results[0]["out"]
```
